# Optimizing a Trainium2 kernel written in Bass

```python
import numpy as np
import jax
import jax.numpy as jnp

def _softmax(x, axis=-1):
    return jax.nn.softmax(x, axis=axis)

def _gelu(x):
    return jax.nn.gelu(x, approximate=True)

def _silu(x):
    return jax.nn.silu(x)

def _sigmoid(x):
    return jax.nn.sigmoid(x)

def _layernorm(x, axis=-1, eps=1e-05):
    m = jnp.mean(x, axis=axis, keepdims=True)
    v = jnp.var(x, axis=axis, keepdims=True)
    return (x - m) / jnp.sqrt(v + eps)

def _scatter_add(tgt, idx, src, axis=0):
    return tgt.at[idx].add(src)

def _segment_sum(src, seg, n):
    return jax.ops.segment_sum(src, seg, n)
kernel_name = 'mk_decoder_postln_d2_seqx_r2_0e640f'

def setup_inputs(seed: int=0):
    np.random.seed(seed)
    _w = jnp.asarray

    def _rec_inputs():
        import jax
        import jax.numpy as jnp
        _rk = jax.random.key(seed)
        x = 7.22e-05 + 1 * jax.random.normal(jax.random.fold_in(_rk, 1), (8, 100, 512), jnp.float32)
        _lenS = 100 - jax.random.randint(jax.random.fold_in(_rk, 7), (8,), 0, max(1, 100 // 4) + 1, jnp.int32)
        _lenS2 = 722 - jax.random.randint(jax.random.fold_in(_rk, 8), (8,), 0, max(1, 722 // 4) + 1, jnp.int32)
        _ctx_1024P = jax.random.normal(jax.random.fold_in(_rk, 11), (8, 16, 512), jnp.float32)
        _ctx_1024c = jax.random.dirichlet(jax.random.fold_in(_rk, 511), 0.3 * jnp.ones((16,), jnp.float32), (8, 722))
        _ctx_1024t = jnp.einsum('bsk,bkd->bsd', _ctx_1024c, _ctx_1024P)
        _ctx_1024t = _ctx_1024t * jax.lax.rsqrt(jnp.mean(jnp.square(_ctx_1024t)) + 1e-12) * 0.953939
        ctx_1024 = 4.13588e-05 + 0.999923 * (_ctx_1024t + 0.3 * jax.random.normal(jax.random.fold_in(_rk, 611), (8, 722, 512), jnp.float32))
        return (x, ctx_1024)
    x, ctx_1024 = _rec_inputs()

    def _L0_attn_setup():
        import jax, jax.numpy as jnp
        import numpy as np
        import math
        N_HEAD = 16
        N_EMBD = 512
        HEAD_D = N_EMBD // N_HEAD
        BASE = 5000

        def rope(Y):
            d = Y.shape[-1]
            t = Y.shape[-2]
            theta = BASE ** (-2.0 * jnp.arange(d // 2, dtype=Y.dtype) / d)
            theta2 = jnp.concatenate([theta, theta], axis=0)
            pos = jnp.arange(1, t + 1, dtype=Y.dtype)
            C = pos[:, None] * theta2[None, :]
            cos, sin = (jnp.cos(C), jnp.sin(C))
            Y2 = jnp.concatenate([-Y[..., d // 2:], Y[..., :d // 2]], axis=-1)
            return Y * cos + Y2 * sin
        key = jax.random.key(seed)
        ks = jax.random.split(key, 9)
        s = 0.02
        x = jax.random.normal(ks[0], (4, 1024, N_EMBD), dtype=jnp.float32)
        Wq = jax.random.normal(ks[1], (N_EMBD, N_EMBD), dtype=jnp.float32) * s
        bq = jnp.zeros((N_EMBD,), dtype=jnp.float32)
        Wk = jax.random.normal(ks[2], (N_EMBD, N_EMBD), dtype=jnp.float32) * s
        bk = jnp.zeros((N_EMBD,), dtype=jnp.float32)
        Wv = jax.random.normal(ks[3], (N_EMBD, N_EMBD), dtype=jnp.float32) * s
        bv = jnp.zeros((N_EMBD,), dtype=jnp.float32)
        Wo = jax.random.normal(ks[4], (N_EMBD, N_EMBD), dtype=jnp.float32) * s
        bo = jnp.zeros((N_EMBD,), dtype=jnp.float32)
        return {'x': x, 'Wq': Wq, 'bq': bq, 'Wk': Wk, 'bk': bk, 'Wv': Wv, 'bv': bv, 'Wo': Wo, 'bo': bo}
    _L0_attn_all = _L0_attn_setup()
    _L0_attn_in = {k: v for k, v in _L0_attn_all.items() if k in ('Wq', 'bq', 'Wk', 'bk', 'Wv', 'bv', 'Wo', 'bo')}
    del _L0_attn_all

    def _L0_xattn_setup():
        import jax, jax.numpy as jnp
        import numpy as np
        B, S, H = (4, 1024, 512)
        key = jax.random.key(seed)
        ks = jax.random.split(key, 6)
        scale = 1.0 / np.sqrt(H)
        return {'query': jax.random.normal(ks[0], (B, S, H), dtype=jnp.float32), 'key': jax.random.normal(ks[1], (B, S, H), dtype=jnp.float32), 'value': jax.random.normal(ks[2], (B, S, H), dtype=jnp.float32), 'WQ': jax.random.normal(ks[3], (H, H), dtype=jnp.float32) * scale, 'WK': jax.random.normal(ks[4], (H, H), dtype=jnp.float32) * scale, 'WV': jax.random.normal(ks[5], (H, H), dtype=jnp.float32) * scale}
    _L0_xattn_all = _L0_xattn_setup()
    _L0_xattn_in = {k: v for k, v in _L0_xattn_all.items() if k in ('WQ', 'WK', 'WV')}
    del _L0_xattn_all

    def _L0_ffn_setup():
        import jax, jax.numpy as jnp
        import numpy as np
        K = 2
        key = jax.random.key(seed)
        ks = jax.random.split(key, 9)
        B, S, D, O, E = (4, 512, 512, 512, 8)
        sc = 0.02
        return {'x': jax.random.normal(ks[0], (B, S, D), dtype=jnp.float32), 'gate_w': jax.random.normal(ks[1], (D, E), dtype=jnp.float32) * sc, 'gate_b': jax.random.normal(ks[2], (E,), dtype=jnp.float32) * sc, 'w1': jax.random.normal(ks[3], (E, D, O), dtype=jnp.float32) * sc, 'b1': jax.random.normal(ks[4], (E, O), dtype=jnp.float32) * sc, 'w2': jax.random.normal(ks[5], (E, O, O), dtype=jnp.float32) * sc, 'b2': jax.random.normal(ks[6], (E, O), dtype=jnp.float32) * sc, 'w3': jax.random.normal(ks[7], (E, O, O), dtype=jnp.float32) * sc, 'b3': jax.random.normal(ks[8], (E, O), dtype=jnp.float32) * sc}
    _L0_ffn_all = _L0_ffn_setup()
    _L0_ffn_in = {k: v for k, v in _L0_ffn_all.items() if k in ('gate_w', 'gate_b', 'w1', 'b1', 'w2', 'b2', 'w3', 'b3')}
    del _L0_ffn_all

    def _L1_attn_setup():
        import jax, jax.numpy as jnp
        import numpy as np
        D_MODEL = 512
        N_HEADS = 16
        HEAD_DIM = D_MODEL // N_HEADS
        D_LATENT = 128
        LAMBDA_DECAY = 0.01
        TIME_STEP = 0.01
        CLAMP = 10000.0

        def _reference_tuple_inner(x, Wq, Wk, Wv, Wo, W_down_kv, W_up_k, W_up_v):
            B, S, _ = x.shape
            q = x @ Wq
            k = x @ Wk
            v = x @ Wv
            latent_kv = (k + v) @ W_down_kv
            k_rec = latent_kv @ W_up_k
            v_rec = latent_kv @ W_up_v

            def heads(t):
                return t.reshape(B, S, N_HEADS, HEAD_DIM).transpose(0, 2, 1, 3)
            qh, kh, vh = (heads(q), heads(k_rec), heads(v_rec))
            scale = 1.0 / (jnp.sqrt(jnp.float32(D_MODEL)) + 1e-08)
            scores = jnp.einsum('bhqd,bhkd->bhqk', qh, kh) * scale
            scores = jnp.clip(jnp.nan_to_num(scores, nan=-1000000000.0), -CLAMP, CLAMP)
            idx = jnp.arange(S, dtype=jnp.float32)
            decay = jnp.exp(-LAMBDA_DECAY * TIME_STEP * jnp.abs(idx[:, None] - idx[None, :]))
            scores = scores * decay[None, None, :, :]
            scores = jnp.clip(jnp.nan_to_num(scores, nan=-1000000000.0), -CLAMP, CLAMP)
            attn = jax.nn.softmax(scores, axis=-1)
            out = jnp.einsum('bhqk,bhkd->bhqd', attn, vh)
            out = out.transpose(0, 2, 1, 3).reshape(B, S, D_MODEL)
            return (out @ Wo, latent_kv)
        key = jax.random.key(seed)
        ks = jax.random.split(key, 8)
        B, S = (2, 1024)

        def w(k, i, o):
            return jax.random.normal(k, (i, o), dtype=jnp.float32) * 0.02
        return {'x': jax.random.normal(ks[0], (B, S, D_MODEL), dtype=jnp.float32), 'Wq': w(ks[1], D_MODEL, D_MODEL), 'Wk': w(ks[2], D_MODEL, D_MODEL), 'Wv': w(ks[3], D_MODEL, D_MODEL), 'Wo': w(ks[4], D_MODEL, D_MODEL), 'W_down_kv': w(ks[5], D_MODEL, D_LATENT), 'W_up_k': w(ks[6], D_LATENT, D_MODEL), 'W_up_v': w(ks[7], D_LATENT, D_MODEL)}
    _L1_attn_all = _L1_attn_setup()
    _L1_attn_in = {k: v for k, v in _L1_attn_all.items() if k in ('Wq', 'Wk', 'Wv', 'Wo', 'W_down_kv', 'W_up_k', 'W_up_v')}
    del _L1_attn_all

    def _L1_xattn_setup():
        import jax, jax.numpy as jnp
        import numpy as np
        EMBED_DIM = 512
        HIDDEN_DIM = 16 * 64
        SCALE = 64 ** (-0.5)
        key = jax.random.key(seed)
        ks = jax.random.split(key, 12)
        B, S = (4, 1024)
        std_in = EMBED_DIM ** (-0.5)
        std_h = HIDDEN_DIM ** (-0.5)
        return {'query': jax.random.normal(ks[0], (B, S, EMBED_DIM), jnp.float32), 'key': jax.random.normal(ks[1], (B, S, EMBED_DIM), jnp.float32), 'value': jax.random.normal(ks[2], (B, S, EMBED_DIM), jnp.float32), 'Wq': jax.random.normal(ks[3], (HIDDEN_DIM, EMBED_DIM), jnp.float32) * std_in, 'bq': jnp.zeros((HIDDEN_DIM,), jnp.float32), 'Wk': jax.random.normal(ks[4], (HIDDEN_DIM, EMBED_DIM), jnp.float32) * std_in, 'bk': jnp.zeros((HIDDEN_DIM,), jnp.float32), 'Wv': jax.random.normal(ks[5], (HIDDEN_DIM, EMBED_DIM), jnp.float32) * std_in, 'bv': jnp.zeros((HIDDEN_DIM,), jnp.float32), 'Wo': jax.random.normal(ks[6], (EMBED_DIM, HIDDEN_DIM), jnp.float32) * std_h, 'bo': jnp.zeros((EMBED_DIM,), jnp.float32)}
    _L1_xattn_all = _L1_xattn_setup()
    _L1_xattn_in = {k: v for k, v in _L1_xattn_all.items() if k in ('Wq', 'bq', 'Wk', 'bk', 'Wv', 'bv', 'Wo', 'bo')}
    del _L1_xattn_all

    def _L1_ffn_setup():
        import jax, jax.numpy as jnp
        import numpy as np
        FEATURES = 512
        D_IN = 512

        def fp8_gemm_optimized(x, input_scale, kernel, kernel_scale):
            s_in = input_scale[0]
            s_k = kernel_scale[0]
            x_q = (x.astype(jnp.float32) / s_in).astype(jnp.float8_e4m3fn)
            k_q = (kernel.astype(jnp.float32) / s_k).astype(jnp.float8_e4m3fn)
            y = jnp.dot(x_q.astype(jnp.float32), k_q.astype(jnp.float32), preferred_element_type=jnp.float32)
            return y * (s_in * s_k)
        key = jax.random.key(seed)
        kx, kk, kb = jax.random.split(key, 3)
        x = jax.random.normal(kx, (4, 4096, D_IN), dtype=jnp.float32)
        limit = np.sqrt(6.0 / (D_IN + FEATURES)).astype(np.float32)
        kernel = jax.random.uniform(kk, (D_IN, FEATURES), dtype=jnp.float32, minval=-limit, maxval=limit).astype(jnp.bfloat16)
        input_scale = jnp.ones((1,), dtype=jnp.float32)
        kernel_scale = jnp.ones((1,), dtype=jnp.float32)
        bias = jnp.zeros((FEATURES,), dtype=jnp.bfloat16)
        return {'x': x, 'kernel': kernel, 'input_scale': input_scale, 'kernel_scale': kernel_scale, 'bias': bias}
    _L1_ffn_all = _L1_ffn_setup()
    _L1_ffn_in = {k: v for k, v in _L1_ffn_all.items() if k in ('kernel', 'input_scale', 'kernel_scale', 'bias')}
    del _L1_ffn_all
    return {'x': x, 'ctx_1024': ctx_1024, 'L0_attn_Wq': _L0_attn_in['Wq'], 'L0_attn_bq': _L0_attn_in['bq'], 'L0_attn_Wk': _L0_attn_in['Wk'], 'L0_attn_bk': _L0_attn_in['bk'], 'L0_attn_Wv': _L0_attn_in['Wv'], 'L0_attn_bv': _L0_attn_in['bv'], 'L0_attn_Wo': _L0_attn_in['Wo'], 'L0_attn_bo': _L0_attn_in['bo'], 'L0_xattn_WQ': _L0_xattn_in['WQ'], 'L0_xattn_WK': _L0_xattn_in['WK'], 'L0_xattn_WV': _L0_xattn_in['WV'], 'L0_ffn_gate_w': _L0_ffn_in['gate_w'], 'L0_ffn_gate_b': _L0_ffn_in['gate_b'], 'L0_ffn_w1': _L0_ffn_in['w1'], 'L0_ffn_b1': _L0_ffn_in['b1'], 'L0_ffn_w2': _L0_ffn_in['w2'], 'L0_ffn_b2': _L0_ffn_in['b2'], 'L0_ffn_w3': _L0_ffn_in['w3'], 'L0_ffn_b3': _L0_ffn_in['b3'], 'L1_attn_Wq': _L1_attn_in['Wq'], 'L1_attn_Wk': _L1_attn_in['Wk'], 'L1_attn_Wv': _L1_attn_in['Wv'], 'L1_attn_Wo': _L1_attn_in['Wo'], 'L1_attn_W_down_kv': _L1_attn_in['W_down_kv'], 'L1_attn_W_up_k': _L1_attn_in['W_up_k'], 'L1_attn_W_up_v': _L1_attn_in['W_up_v'], 'L1_xattn_Wq': _L1_xattn_in['Wq'], 'L1_xattn_bq': _L1_xattn_in['bq'], 'L1_xattn_Wk': _L1_xattn_in['Wk'], 'L1_xattn_bk': _L1_xattn_in['bk'], 'L1_xattn_Wv': _L1_xattn_in['Wv'], 'L1_xattn_bv': _L1_xattn_in['bv'], 'L1_xattn_Wo': _L1_xattn_in['Wo'], 'L1_xattn_bo': _L1_xattn_in['bo'], 'L1_ffn_kernel': _L1_ffn_in['kernel'], 'L1_ffn_input_scale': _L1_ffn_in['input_scale'], 'L1_ffn_kernel_scale': _L1_ffn_in['kernel_scale'], 'L1_ffn_bias': _L1_ffn_in['bias']}

def reference(x, ctx_1024, L0_attn_Wq, L0_attn_bq, L0_attn_Wk, L0_attn_bk, L0_attn_Wv, L0_attn_bv, L0_attn_Wo, L0_attn_bo, L0_xattn_WQ, L0_xattn_WK, L0_xattn_WV, L0_ffn_gate_w, L0_ffn_gate_b, L0_ffn_w1, L0_ffn_b1, L0_ffn_w2, L0_ffn_b2, L0_ffn_w3, L0_ffn_b3, L1_attn_Wq, L1_attn_Wk, L1_attn_Wv, L1_attn_Wo, L1_attn_W_down_kv, L1_attn_W_up_k, L1_attn_W_up_v, L1_xattn_Wq, L1_xattn_bq, L1_xattn_Wk, L1_xattn_bk, L1_xattn_Wv, L1_xattn_bv, L1_xattn_Wo, L1_xattn_bo, L1_ffn_kernel, L1_ffn_input_scale, L1_ffn_kernel_scale, L1_ffn_bias):
    import jax
    import jax.numpy as jnp

    def _L0_attn_ref(x, Wq, bq, Wk, bk, Wv, bv, Wo, bo):
        import jax, jax.numpy as jnp
        import numpy as np
        import math
        N_HEAD = 16
        N_EMBD = 512
        HEAD_D = N_EMBD // N_HEAD
        BASE = 5000

        def rope(Y):
            d = Y.shape[-1]
            t = Y.shape[-2]
            theta = BASE ** (-2.0 * jnp.arange(d // 2, dtype=Y.dtype) / d)
            theta2 = jnp.concatenate([theta, theta], axis=0)
            pos = jnp.arange(1, t + 1, dtype=Y.dtype)
            C = pos[:, None] * theta2[None, :]
            cos, sin = (jnp.cos(C), jnp.sin(C))
            Y2 = jnp.concatenate([-Y[..., d // 2:], Y[..., :d // 2]], axis=-1)
            return Y * cos + Y2 * sin
        b, t, _ = x.shape

        def split_heads(y):
            return y.reshape(b, t, N_HEAD, HEAD_D).transpose(0, 2, 1, 3)
        q = split_heads(x @ Wq.T + bq)
        k = split_heads(x @ Wk.T + bk)
        v = split_heads(x @ Wv.T + bv)
        q, k = (rope(q), rope(k))
        scale = math.sqrt(HEAD_D)
        att = jnp.einsum('bhqd,bhkd->bhqk', q, k) / scale
        mask = jnp.tril(jnp.ones((t, t), dtype=bool))
        att = jnp.where(mask, att, -jnp.inf)
        att = jax.nn.softmax(att, axis=-1)
        y = jnp.einsum('bhqk,bhkd->bhqd', att, v)
        y = y.transpose(0, 2, 1, 3).reshape(b, t, N_EMBD)
        return y @ Wo.T + bo

    def _L0_xattn_ref(query, key, value, WQ, WK, WV):
        import jax, jax.numpy as jnp
        import numpy as np
        B, S, H = (4, 1024, 512)
        q = jnp.einsum('bsh,oh->bso', query, WQ)
        k = jnp.einsum('bsh,oh->bso', key, WK)
        v = jnp.einsum('bsh,oh->bso', value, WV)
        hidden_size = q.shape[-1]
        scores = jnp.einsum('bqh,bkh->bqk', q, k) / jnp.sqrt(jnp.float32(hidden_size))
        attn = jax.nn.softmax(scores, axis=2)
        return jnp.einsum('bqk,bkh->bqh', attn, v)

    def _L0_ffn_ref(x, gate_w, gate_b, w1, b1, w2, b2, w3, b3):
        import jax, jax.numpy as jnp
        import numpy as np
        K = 2
        E = gate_w.shape[-1]
        logits = jnp.einsum('bsd,de->bse', x, gate_w) + gate_b
        probs = jax.nn.softmax(logits, axis=1)
        vals, idx = jax.lax.top_k(probs, K)
        h = jax.nn.relu(jnp.einsum('bsd,edo->ebso', x, w1) + b1[:, None, None, :])
        h = jax.nn.relu(jnp.einsum('ebso,eop->ebsp', h, w2) + b2[:, None, None, :])
        y = jax.nn.relu(jnp.einsum('ebso,eop->ebsp', h, w3) + b3[:, None, None, :])
        onehot = jax.nn.one_hot(idx, E, dtype=x.dtype)
        w_tok = jnp.einsum('bske,bsk->bse', onehot, vals)
        ind = onehot.max(axis=2)
        v = jnp.einsum('ebso,bse->eo', y, w_tok)
        out = jnp.einsum('bse,eo->bso', ind, v)
        return out

    def _L1_attn_ref(x, Wq, Wk, Wv, Wo, W_down_kv, W_up_k, W_up_v):
        import jax, jax.numpy as jnp
        import numpy as np
        D_MODEL = 512
        N_HEADS = 16
        HEAD_DIM = D_MODEL // N_HEADS
        D_LATENT = 128
        LAMBDA_DECAY = 0.01
        TIME_STEP = 0.01
        CLAMP = 10000.0

        def _reference_tuple_inner(x, Wq, Wk, Wv, Wo, W_down_kv, W_up_k, W_up_v):
            B, S, _ = x.shape
            q = x @ Wq
            k = x @ Wk
            v = x @ Wv
            latent_kv = (k + v) @ W_down_kv
            k_rec = latent_kv @ W_up_k
            v_rec = latent_kv @ W_up_v

            def heads(t):
                return t.reshape(B, S, N_HEADS, HEAD_DIM).transpose(0, 2, 1, 3)
            qh, kh, vh = (heads(q), heads(k_rec), heads(v_rec))
            scale = 1.0 / (jnp.sqrt(jnp.float32(D_MODEL)) + 1e-08)
            scores = jnp.einsum('bhqd,bhkd->bhqk', qh, kh) * scale
            scores = jnp.clip(jnp.nan_to_num(scores, nan=-1000000000.0), -CLAMP, CLAMP)
            idx = jnp.arange(S, dtype=jnp.float32)
            decay = jnp.exp(-LAMBDA_DECAY * TIME_STEP * jnp.abs(idx[:, None] - idx[None, :]))
            scores = scores * decay[None, None, :, :]
            scores = jnp.clip(jnp.nan_to_num(scores, nan=-1000000000.0), -CLAMP, CLAMP)
            attn = jax.nn.softmax(scores, axis=-1)
            out = jnp.einsum('bhqk,bhkd->bhqd', attn, vh)
            out = out.transpose(0, 2, 1, 3).reshape(B, S, D_MODEL)
            return (out @ Wo, latent_kv)
        return _reference_tuple_inner(x, Wq, Wk, Wv, Wo, W_down_kv, W_up_k, W_up_v)[0]

    def _L1_xattn_ref(query, key, value, Wq, bq, Wk, bk, Wv, bv, Wo, bo):
        import jax, jax.numpy as jnp
        import numpy as np
        EMBED_DIM = 512
        HIDDEN_DIM = 16 * 64
        SCALE = 64 ** (-0.5)
        q = jnp.einsum('bsd,hd->bsh', query, Wq) + bq
        k = jnp.einsum('bsd,hd->bsh', key, Wk) + bk
        v = jnp.einsum('bsd,hd->bsh', value, Wv) + bv
        scores = jnp.einsum('bqh,bkh->bqk', q, k) * SCALE
        attn = jax.nn.softmax(scores, axis=1)
        out = jnp.einsum('bqk,bkh->bqh', attn, v)
        return jnp.einsum('bqh,dh->bqd', out, Wo) + bo

    def _L1_ffn_ref(x, kernel, input_scale, kernel_scale, bias):
        import jax, jax.numpy as jnp
        import numpy as np
        FEATURES = 512
        D_IN = 512

        def fp8_gemm_optimized(x, input_scale, kernel, kernel_scale):
            s_in = input_scale[0]
            s_k = kernel_scale[0]
            x_q = (x.astype(jnp.float32) / s_in).astype(jnp.float8_e4m3fn)
            k_q = (kernel.astype(jnp.float32) / s_k).astype(jnp.float8_e4m3fn)
            y = jnp.dot(x_q.astype(jnp.float32), k_q.astype(jnp.float32), preferred_element_type=jnp.float32)
            return y * (s_in * s_k)
        dtype = jnp.bfloat16
        x = x.astype(dtype)
        orig_shape = x.shape
        x2 = x.reshape(-1, x.shape[-1])
        y = fp8_gemm_optimized(x2, input_scale, kernel, kernel_scale)
        y = y.astype(dtype) + bias
        return y.reshape(orig_shape[:-1] + (FEATURES,))
    x = _layernorm(x + _L0_attn_ref(x, L0_attn_Wq, L0_attn_bq, L0_attn_Wk, L0_attn_bk, L0_attn_Wv, L0_attn_bv, L0_attn_Wo, L0_attn_bo), axis=-1)
    x = _layernorm(x + _L0_xattn_ref(x, ctx_1024, ctx_1024, L0_xattn_WQ, L0_xattn_WK, L0_xattn_WV), axis=-1)
    x = _layernorm(x + _L0_ffn_ref(x, L0_ffn_gate_w, L0_ffn_gate_b, L0_ffn_w1, L0_ffn_b1, L0_ffn_w2, L0_ffn_b2, L0_ffn_w3, L0_ffn_b3), axis=-1)
    x = _layernorm(x + _L1_attn_ref(x, L1_attn_Wq, L1_attn_Wk, L1_attn_Wv, L1_attn_Wo, L1_attn_W_down_kv, L1_attn_W_up_k, L1_attn_W_up_v), axis=-1)
    x = _layernorm(x + _L1_xattn_ref(x, ctx_1024, ctx_1024, L1_xattn_Wq, L1_xattn_bq, L1_xattn_Wk, L1_xattn_bk, L1_xattn_Wv, L1_xattn_bv, L1_xattn_Wo, L1_xattn_bo), axis=-1)
    x = _layernorm(x + _L1_ffn_ref(x, L1_ffn_kernel, L1_ffn_input_scale, L1_ffn_kernel_scale, L1_ffn_bias), axis=-1)
    return x

_drawn_inputs = setup_inputs


def setup_inputs(seed=0):
    import zlib

    import numpy as np

    out = dict(_drawn_inputs(seed))
    spreads = {'L0_attn_bq': (0.0, 0.8),
     'L0_attn_bk': (0.0, 0.8),
     'L0_attn_bv': (0.0, 0.1),
     'L0_attn_bo': (0.0, 0.1),
     'L1_xattn_bq': (0.0, 0.8),
     'L1_xattn_bk': (0.0, 0.1),
     'L1_xattn_bv': (0.0, 0.1),
     'L1_xattn_bo': (0.0, 0.1)}
    factors = {'L0_attn_Wq': 3.077,
     'L0_ffn_gate_b': 8.0,
     'L0_ffn_b1': 6.743,
     'L0_ffn_b2': 2.858,
     'L1_attn_Wq': 8.0,
     'L1_attn_Wk': 4.818,
     'L1_attn_Wv': 5.015,
     'L1_attn_Wo': 4.15,
     'L1_attn_W_down_kv': 4.029,
     'L1_attn_W_up_k': 8.0,
     'L1_attn_W_up_v': 4.008}
    for name, (base, spread) in spreads.items():
        noise = np.random.default_rng([zlib.crc32(name.encode()), seed]).standard_normal(out[name].shape)
        drawn = base * np.exp(spread * noise) if base else spread * noise
        out[name] = jnp.asarray(drawn.astype(out[name].dtype))
    for name, factor in factors.items():
        out[name] = (out[name] * factor).astype(out[name].dtype)
    return out
```

```python
from contextlib import ExitStack

import numpy as np

import concourse.bass as bass
from concourse import mybir

ALU = mybir.AluOpType
ACT = mybir.ActivationFunctionType
AX = mybir.AxisListType
F32 = mybir.dt.float32
FR = mybir.dt.float32r
BF16 = mybir.dt.bfloat16
I32 = mybir.dt.int32
U32 = mybir.dt.uint32

P = 128
B, T, D = 8, 100, 512
S = 722
NH, HD = 16, 32
C = D // P
HPC = P // HD
N = B * T
HALF = N // 2
KT = -(-S // P)
LAST = S - (KT - 1) * P
HID = 1024
HC = HID // P
E = 8
LAT = 128
EPS = 1e-5
CLAMP = 10000.0
VW = HD + 2

ROWS = {"L0_attn_bq": 0, "L0_attn_bk": 1, "L0_attn_bv": 2, "L1_xattn_bq": 3, "L1_xattn_bk": 5,
        "L1_xattn_bv": 7, "L0_ffn_b1": 9, "L0_ffn_b2": 17, "L0_ffn_b3": 25}
NROWS = 33


def constants():
    f = np.float32
    theta = (f(5000.0) ** (f(-2.0) * np.arange(HD // 2, dtype=f) / f(HD))).astype(f)
    theta = np.tile(np.concatenate([theta, theta]), HPC)
    angle = (np.arange(1, T + 1, dtype=f)[None, :] * theta[:, None]).astype(f)
    rot = np.zeros((P, P), f)
    for h in range(HPC):
        for d in range(HD // 2):
            rot[h * HD + d + HD // 2, h * HD + d] = -1.0
            rot[h * HD + d, h * HD + d + HD // 2] = 1.0
    q = np.arange(T)
    causal = np.where(q[None, :] <= q[:, None], 0.0, -1e30).astype(f)
    decay = np.exp(f(-0.01 * 0.01) * np.abs(q[:, None] - q[None, :]).astype(f)).astype(f)
    return {"ident": np.eye(P, dtype=f), "cos": np.cos(angle), "sin": np.sin(angle), "rot": rot,
            "causal": np.tile(causal, (1, 4)), "decay": decay,
            "iota8": np.tile(np.arange(E, dtype=f), (P, 1))}


def three(aH, aL, bH, bL):
    return [(aH, bH), (aH, bL), (aL, bH)]


class Pair:

    def __init__(self, hi, lo):
        self.hi, self.lo = hi, lo

    def __getitem__(self, key):
        return Pair(self.hi[key], self.lo[key])


def times(a, b):
    return three(a.hi, a.lo, b.hi, b.lo)


def emit_products(pe, out, products):
    for n, (a, b) in enumerate(products):
        last = pe.matmul(out, a, b, start=(n == 0), stop=(n == len(products) - 1))
    return last


def program(nc, g, out, debug=None):
    ctx = ExitStack()
    with ctx:
        def sb(name, shape, dt=F32, where=ctx):
            return where.enter_context(nc.sbuf_tensor(name, shape, dt))

        def pair(name, shape, where=ctx):
            return Pair(sb(name + "_hi", shape, FR, where), sb(name + "_lo", shape, FR, where))

        held = []

        def sem(name):
            held.append(nc.alloc_semaphore(name=name))
            return held[-1]

        def free_semaphores():
            nc.clear_and_free_semaphores(held)
            nc.all_engine_barrier()
            held.clear()

        ps = ctx.enter_context(nc.psum_tensor("ps", [P, 8, 512], F32))
        ident = sb("ident", [P, P])
        identR = sb("identR", [P, P], FR)
        BT = sb("bias_turned", [P, C, NROWS])
        x = sb("x", [P, B, D])
        xT = pair("xT", [P, C, N])
        stats = sb("stats", [P, B, 6])
        mv = sb("mean_var", [P, B, 2])
        rstd = sb("rstd", [P, B])
        bo_rows = sb("bo_rows", [P, D])

        def turn_stage(name, jobs, copy_only=False):
            pass

        def product_stage(name, jobs, banks=8, first=0, extra=None):
            filled, hi_done, lo_done = sem(name + "_filled"), sem(name + "_hi"), sem(name + "_lo")
            with nc.Block() as block:
                @block.tensor
                def _(pe):
                    for n, (emit, view, *_r) in enumerate(jobs):
                        if n >= banks:
                            pe.wait_ge(lo_done, n - banks + 1)
                        emit(nc.tensor, view(ps[:, first + n % banks, :])).then_inc(filled, 1)

                @block.scalar
                def _(act):
                    for n, (emit, view, dst, bias, scale) in enumerate(jobs):
                        act.wait_ge(filled, n + 1)
                        src = view(ps[:, first + n % banks, :])
                        to = dst.hi if isinstance(dst, Pair) else dst
                        nc.scalar.activation(to, src, ACT.Identity, bias=0.0 if bias is None else bias,
                                             scale=scale).then_inc(hi_done, 1)

                @block.vector
                def _(dve):
                    for n, (emit, view, dst, bias, scale) in enumerate(jobs):
                        dve.wait_ge(hi_done, n + 1)
                        if not isinstance(dst, Pair):
                            if n:
                                dve.wait_ge(lo_done, n)
                            dve.sem_inc(lo_done, 1)
                            continue
                        src = view(ps[:, first + n % banks, :])
                        if scale != 1.0:
                            assert bias is None
                            nc.vector.scalar_tensor_tensor(dst.lo, src, scale, dst.hi.bitcast(F32),
                                                           ALU.mult, ALU.subtract).then_inc(lo_done, 1)
                        elif bias is not None:
                            nc.vector.scalar_tensor_tensor(dst.lo, src, bias, dst.hi.bitcast(F32),
                                                           ALU.add, ALU.subtract).then_inc(lo_done, 1)
                        else:
                            nc.vector.tensor_tensor(dst.lo, src, dst.hi.bitcast(F32),
                                                    ALU.subtract).then_inc(lo_done, 1)

        def turn_job(blocks, rows, cols, dst, bias=None):
            def emit(pe, bank):
                for col, src in blocks:
                    k, m = src.shape[0], src.shape[-1]
                    last = pe.transpose(bank[0:m, col:col + k], src, ident[0:k, 0:k])
                return last
            return (lambda pe, v: emit(pe, v), lambda bank: bank, dst, bias, 1.0, rows, cols)

        def jobs_of(turns):
            res = []
            for emit, _v, dst, bias, scale, rows, cols in turns:
                res.append((emit, rows, cols, dst, bias, scale))
            return res

        def tile_job(products, dst, rows=P, cols=HALF, bias=None, scale=1.0):
            return (lambda pe, bank: emit_products(pe, bank, products),
                    lambda bank: bank[0:rows, 0:cols], dst, bias, scale)

        def flip_job(blocks, dst, rows=P, cols=512, bias=None):
            def emit(pe, bank):
                for col, src in blocks:
                    k, m = src.shape[0], src.shape[-1]
                    last = pe.transpose(bank[0:m, col:col + k], src, ident[0:k, 0:k])
                return last
            return (emit, lambda bank: bank[0:rows, 0:cols], dst, bias, 1.0)

        def turn_weight(w, dst, nrow=C, ncol=C):
            res = []
            for c in range(ncol):
                for r0 in range(0, nrow, 4):
                    rn = min(4, nrow - r0)
                    res.append(flip_job([(k * P, w[:, r0 + k, c * P:(c + 1) * P]) for k in range(rn)],
                                        dst[:, c, r0 * P:(r0 + rn) * P], cols=rn * P))
            return res

        def project(wT, src, dst, bias=None, scale=1.0, kc=C, mc=C):
            res = []
            for m in range(mc):
                for h in range(2):
                    products = []
                    for k in range(kc):
                        products += times(wT[:, k, m * P:(m + 1) * P],
                                          src[:, k, h * HALF:(h + 1) * HALF])
                    res.append(tile_job(products, dst[:, m, h * HALF:(h + 1) * HALF],
                                        bias=None if bias is None else bias(m), scale=scale))
            return res

        def split_stage(name, items):
            hi_done, lo_done = sem(name + "_hi"), sem(name + "_lo")
            with nc.Block() as block:
                @block.scalar
                def _(act):
                    for to, src in items:
                        nc.scalar.activation(to.hi, src, ACT.Identity).then_inc(hi_done, 1)

                @block.vector
                def _(dve):
                    for n, (to, src) in enumerate(items):
                        dve.wait_ge(hi_done, n + 1)
                        nc.vector.tensor_tensor(to.lo, src, to.hi.bitcast(F32),
                                                ALU.subtract).then_inc(lo_done, 1)

        def load_stage(name, loads):
            landed = sem(name)
            with nc.Block() as block:
                @block.sync
                def _(sp):
                    for dst, src in loads:
                        sp.dma_start(dst, src).then_inc(landed, 16)
                    sp.wait_ge(landed, 16 * len(loads))

        def norm_stage(name, emit, residual, gain=None, turned=True, z=None, last=False):
            made, added, stat, aggr, scaled = (sem(f"{name}_{s}") for s in
                                               ("made", "added", "stat", "aggr", "scaled"))
            rooted, normed, turned_s, hi_done, lo_done = (
                sem(f"{name}_{s}") for s in ("rooted", "normed", "turned", "hi", "lo"))
            with nc.Block() as block:
                @block.tensor
                def _(pe):
                    def flips(b):
                        pe.wait_ge(normed, b + 1)
                        if b >= 2:
                            pe.wait_ge(lo_done, b - 1)
                        for c in range(C):
                            mm = nc.tensor.transpose(ps[:, 4 + b % 2, c * T:(c + 1) * T],
                                                     x[0:T, b, c * P:(c + 1) * P], ident[0:T, 0:T])
                        mm.then_inc(turned_s, 1)

                    for b in range(B):
                        if b >= 4:
                            pe.wait_ge(added, b - 3)
                        emit(nc.tensor, ps[0:T, b % 4, :], b).then_inc(made, 1)
                        if turned and b >= 2:
                            flips(b - 2)
                    if turned:
                        flips(B - 2)
                        flips(B - 1)

                @block.vector
                def _(dve):
                    def first(b):
                        dve.wait_ge(made, b + 1)
                        if gain is None:
                            nc.vector.tensor_tensor(x[0:T, b, :], ps[0:T, b % 4, :], residual[0:T, b, :],
                                                    ALU.add).then_inc(added, 1)
                        else:
                            col, rows = gain(b)
                            nc.vector.scalar_tensor_tensor(z[0:T, b % 2, :], rows, col, ps[0:T, b % 4, :],
                                                           ALU.mult, ALU.add).then_inc(aggr, 0 + 1)
                            dve.wait_ge(aggr, 2 * b + 1)
                            nc.vector.tensor_tensor(x[0:T, b, :], z[0:T, b % 2, :], residual[0:T, b, :],
                                                    ALU.add).then_inc(added, 1)
                        dve.wait_ge(added, b + 1)
                        nc.vector.bn_stats(stats[0:T, b, :], x[0:T, b, :]).then_inc(stat, 1)
                        dve.wait_ge(stat, b + 1)
                        nc.vector.bn_aggr(mv[0:T, b, :], stats[0:T, b, :]).then_inc(aggr, 1)

                    def second(b):
                        dve.wait_ge(rooted, 2 * b + 2)
                        nc.vector.tensor_scalar(x[0:T, b, :], x[0:T, b, :], mv[0:T, b, 0:1], rstd[0:T, b:b + 1],
                                                ALU.subtract, ALU.mult).then_inc(normed, 1)

                    def third(b):
                        dve.wait_ge(hi_done, b + 1)
                        nc.vector.tensor_tensor(xT.lo[:, :, b * T:(b + 1) * T],
                                                ps[:, 4 + b % 2, 0:C * T].rearrange("p (c t) -> p c t", c=C),
                                                xT.hi[:, :, b * T:(b + 1) * T].bitcast(F32),
                                                ALU.subtract).then_inc(lo_done, 1)

                    for b in range(B + 3):
                        if b < B:
                            first(b)
                        if 1 <= b <= B:
                            second(b - 1)
                        if turned and b >= 3:
                            third(b - 3)

                @block.gpsimd
                def _(pool):
                    per = 2 if gain is not None else 1
                    for b in range(B):
                        pool.wait_ge(aggr, per * (b + 1))
                        nc.gpsimd.tensor_scalar(rstd[0:T, b:b + 1], mv[0:T, b, 1:2], EPS, None,
                                                ALU.add).then_inc(rooted, 1)
                        pool.wait_ge(rooted, 2 * b + 1)
                        nc.gpsimd.tensor_tensor(rstd[0:T, b:b + 1], rstd[0:T, b:b + 1], minus_half[0:T, :],
                                                ALU.pow).then_inc(rooted, 1)

                @block.scalar
                def _(act):
                    if turned:
                        for b in range(B):
                            act.wait_ge(turned_s, b + 1)
                            nc.scalar.activation(xT.hi[:, :, b * T:(b + 1) * T],
                                                 ps[:, 4 + b % 2, 0:C * T].rearrange("p (c t) -> p c t", c=C),
                                                 ACT.Identity).then_inc(hi_done, 1)

                @block.sync
                def _(sp):
                    if last:
                        for b in range(B):
                            sp.wait_ge(normed, b + 1)
                            sp.dma_start(out[b], x[0:T, b, :]).then_inc(scaled, 16)
                        sp.wait_ge(scaled, 16 * B)

        minus_half = sb("minus_half", [P, 1])

        def dump(name):
            if debug is not None and name in debug:
                done = sem("dump_" + name)
                with nc.Block() as block:
                    @block.sync
                    def _(sp):
                        for b in range(B):
                            sp.dma_start(debug[name][b], x[0:T, b, :]).then_inc(done, 16)
                        sp.wait_ge(done, 16 * B)

        hid = lambda a: a.rearrange("(c p) d -> p c d", p=P)
        natural = lambda w, r=C: w.rearrange("(r p) i -> p r i", p=P)

        start = ExitStack()
        rows = sb("bias_rows", [NROWS, D], F32, start)
        loads = [(ident[:], g["ident"]), (bo_rows[:], g["L0_attn_bo"].partition_broadcast(P))]
        for key, at in ROWS.items():
            v = g[key]
            n = v.shape[0] if len(v.shape) == 2 else v.shape[0] // D
            if len(v.shape) == 1:
                v = v.rearrange("(r i) -> r i", i=D)
            loads.append((rows[at:at + n, :], v))
        for b in range(B):
            loads.append((x[0:T, b, :], g["x"][b]))
        load_stage("ld_start", loads)
        started = sem("started")
        with nc.Block() as block:
            @block.vector
            def _(dve):
                nc.vector.memset(minus_half[:], -0.5).then_inc(started, 1)
                nc.vector.tensor_copy(identR[:], ident[:]).then_inc(started, 1)

        jobs = [flip_job([(c * NROWS, rows[:, c * P:(c + 1) * P]) for c in range(C)],
                         BT[:, :, :].rearrange("p c r -> p (c r)"), cols=C * NROWS)]
        for b in range(B):
            jobs.append(flip_job([(c * T, x[0:T, b, c * P:(c + 1) * P]) for c in range(C)],
                                 xT[:, :, b * T:(b + 1) * T], cols=C * T))
        jobs = [jobs[0]] + [(e, (lambda bank: bank[:, 0:C * T].rearrange("p (c t) -> p c t", c=C)), d, bi, s)
                            for e, v, d, bi, s in jobs[1:]]
        fixed = []
        for e, v, d, bi, s in jobs:
            fixed.append(((lambda pe, view, e=e: e(pe, view)), v, d, bi, s))
        jobs = [fixed[0]]
        for b in range(B):
            def emit(pe, view, b=b):
                for c in range(C):
                    last = pe.transpose(view[:, c, :], x[0:T, b, c * P:(c + 1) * P], ident[0:T, 0:T])
                return last
            jobs.append((emit, lambda bank: bank[:, 0:C * T].rearrange("p (c t) -> p c t", c=C),
                         xT[:, :, b * T:(b + 1) * T], None, 1.0))
        product_stage("turn_x", jobs)
        start.close()

        def add_rows_stage(name):
            done = sem(name)
            with nc.Block() as block:
                @block.gpsimd
                def _(pool):
                    for b in range(B):
                        nc.gpsimd.tensor_tensor(x[0:T, b, :], x[0:T, b, :], bo_rows[0:T, :],
                                                ALU.add).then_inc(done, 1)

        def load_turned(name, keys, phase, stack):
            raw = [sb(f"{name}_raw{i}", [P, C, D], F32, stack) for i in range(len(keys))]
            dst = [pair(f"{name}_w{i}", [P, C, D], phase) for i in range(len(keys))]
            return raw, dst

        def attention_stage(name, qT, kT, v, yT, scale, masked, decay, phase):
            E_ = sb(name + "_e", [T, 2, HPC, C, T], F32, phase)
            mx = sb(name + "_mx", [T, 2, HPC, C], F32, phase)
            aT = pair(name + "_aT", [T, 2, HPC * C, T], phase)
            rec = sb(name + "_rec", [T, 2, NH], F32, phase)
            y = sb(name + "_y", [T, 2, NH, HD], F32, phase)
            sc, red, ex, tp, thi, tlo, pv, yn, clip = (sem(f"{name}_{s}") for s in (
                "scores", "max", "exp", "turned", "thi", "tlo", "pv", "y", "clip"))
            sub, rc = sem(name + "_sub"), sem(name + "_rec")
            with nc.Block() as block:
                @block.tensor
                def _(pe):
                    def scores(b):
                        if b >= 1:
                            pe.wait_ge(clip if decay is not None else sub, b)
                        for r in range(HPC):
                            if masked:
                                nc.tensor.matmul(ps[0:T, r, 0:C * T], identR[0:T, 0:T], causal[:, :],
                                                 start=True, stop=False, skip_group_check=True)
                        for c in range(C):
                            for r in range(HPC):
                                mm = nc.tensor.matmul(
                                    ps[0:T, r, c * T:(c + 1) * T],
                                    qT[r * HD:(r + 1) * HD, c, b * T:(b + 1) * T],
                                    kT[r * HD:(r + 1) * HD, c, b * T:(b + 1) * T],
                                    start=not masked, stop=True, skip_group_check=True)
                        mm.then_inc(sc, 1)

                    def turn(b):
                        pe.wait_ge(ex, b + 1)
                        for r in range(HPC):
                            n = 5 * b + r
                            if n >= 2:
                                pe.wait_ge(tlo, n - 1)
                            for c in range(C):
                                mm = nc.tensor.transpose(ps[0:T, 4 + n % 2, c * T:(c + 1) * T],
                                                         E_[:, b % 2, r, c, :], ident[0:T, 0:T])
                            mm.then_inc(tp, 1)

                    def values(b):
                        pe.wait_ge(tlo, 5 * b + 4)
                        if b >= 1:
                            pe.wait_ge(yn, b)
                        for h in range(NH):
                            r, c = h % HPC, h // HPC
                            w = aT[:, b % 2, r * C + c, :]
                            mm = emit_products(nc.tensor, ps[0:T, 6 + h // 8, h % 8 * VW:(h % 8 + 1) * VW],
                                               times(w, v[:, b, h, :]))
                        mm.then_inc(pv, 1)

                    def turn_y(b):
                        n = 5 * b + 4
                        pe.wait_ge(yn, b + 1)
                        pe.wait_ge(tlo, n - 1)
                        for c in range(C):
                            mm = nc.tensor.transpose(
                                ps[:, 4 + n % 2, c * T:(c + 1) * T],
                                y[:, b % 2, c * HPC:(c + 1) * HPC, :].rearrange("t h d -> t (h d)"),
                                ident[0:T, 0:T])
                        mm.then_inc(tp, 1)

                    scores(0)
                    for b in range(B):
                        turn(b)
                        if b + 1 < B:
                            scores(b + 1)
                        values(b)
                        turn_y(b)

                @block.vector
                def _(dve):
                    def soft(b):
                        s, wide = ps[0:T, 0:HPC, 0:C * T], "q r (c k) -> q r c k"
                        src = s.rearrange(wide, c=C)
                        dve.wait_ge(sc, b + 1)
                        if b >= 2:
                            dve.wait_ge(tp, 5 * (b - 2) + 4)
                        if decay is not None:
                            nc.vector.tensor_scalar(E_[:, b % 2, :, :, :].rearrange("q r c k -> q r (c k)"), s,
                                                    -CLAMP, CLAMP, ALU.max, ALU.min).then_inc(clip, 1)
                            dve.wait_ge(clip, b + 1)
                            e = E_[:, b % 2, :, :, :].rearrange("q r c k -> q (r c) k")
                            nc.vector.tensor_tensor(
                                e, e, decay[:, :].unsqueeze(1).to_broadcast([T, NH, T]), ALU.mult
                            ).then_inc(sub, 1)
                            dve.wait_ge(sub, 2 * b + 1)
                            nc.vector.tensor_reduce(mx[:, b % 2, :, :].rearrange("q r c -> q (r c)"), e,
                                                    AX.X, ALU.max).then_inc(red, 1)
                            dve.wait_ge(red, b + 1)
                            m = mx[:, b % 2, :, :].rearrange("q r c -> q (r c)").unsqueeze(2)
                            nc.vector.tensor_tensor(e, e, m.to_broadcast([T, NH, T]),
                                                    ALU.subtract).then_inc(sub, 1)
                        else:
                            nc.vector.tensor_reduce(mx[:, b % 2, :, :], src, AX.X, ALU.max).then_inc(red, 1)
                            dve.wait_ge(red, b + 1)
                            for r in range(HPC):
                                ins = nc.vector.tensor_tensor(
                                    E_[:, b % 2, r, :, :], src[:, r, :, :],
                                    mx[:, b % 2, r, :].unsqueeze(2).to_broadcast([T, C, T]), ALU.subtract)
                            ins.then_inc(sub, 1)

                    def lows(b, k):
                        n = 5 * b + k
                        dve.wait_ge(thi, n + 1)
                        if k < HPC:
                            to = aT[:, b % 2, k * C:(k + 1) * C, :]
                            src = ps[0:T, 4 + n % 2, 0:C * T]
                        else:
                            to = yT[:, :, b * T:(b + 1) * T]
                            src = ps[:, 4 + n % 2, 0:C * T]
                        src = src.rearrange("p (c t) -> p c t", c=C)
                        if k < HPC or bias_of is None:
                            nc.vector.tensor_tensor(to.lo, src, to.hi.bitcast(F32), ALU.subtract).then_inc(tlo, 1)
                        else:
                            for c in range(C):
                                ins = nc.vector.scalar_tensor_tensor(
                                    to.lo[:, c, :], src[:, c, :], bias_of(c), to.hi[:, c, :].bitcast(F32),
                                    ALU.add, ALU.subtract)
                            ins.then_inc(tlo, 1)

                    def outputs(b):
                        dve.wait_ge(pv, b + 1)
                        for h in range(2):
                            o = ps[0:T, 6 + h, 0:8 * VW].rearrange("q (h d) -> q h d", h=8)
                            ins = nc.vector.reciprocal(rec[:, b % 2, 8 * h:8 * h + 8].unsqueeze(2), o[:, :, HD:HD + 1])
                        ins.then_inc(rc, 1)
                        dve.wait_ge(rc, b + 1)
                        if b >= 2:
                            dve.wait_ge(tp, 5 * (b - 2) + 5)
                        for h in range(2):
                            o = ps[0:T, 6 + h, 0:8 * VW].rearrange("q (h d) -> q h d", h=8)
                            ins = nc.vector.tensor_tensor(
                                y[:, b % 2, 8 * h:8 * h + 8, :], o[:, :, 0:HD],
                                rec[:, b % 2, 8 * h:8 * h + 8].unsqueeze(2).to_broadcast([T, 8, HD]), ALU.mult)
                        ins.then_inc(yn, 1)

                    soft(0)
                    for b in range(B):
                        for k in range(HPC):
                            lows(b, k)
                        if b + 1 < B:
                            soft(b + 1)
                        outputs(b)
                        lows(b, HPC)

                @block.scalar
                def _(act):
                    def expo(b):
                        act.wait_ge(sub, (2 if decay is not None else 1) * (b + 1))
                        e = E_[:, b % 2, :, :, :].rearrange("q r c k -> q (r c k)")
                        nc.scalar.activation(e, e, ACT.Exp, scale=scale).then_inc(ex, 1)

                    def highs(b, k):
                        n = 5 * b + k
                        act.wait_ge(tp, n + 1)
                        if k < HPC:
                            if b >= 2 and k == 0:
                                act.wait_ge(pv, b - 1)
                            to = aT.hi[:, b % 2, k * C:(k + 1) * C, :]
                            src = ps[0:T, 4 + n % 2, 0:C * T]
                        else:
                            to = yT.hi[:, :, b * T:(b + 1) * T]
                            src = ps[:, 4 + n % 2, 0:C * T]
                        src = src.rearrange("p (c t) -> p c t", c=C)
                        if k < HPC or bias_of is None:
                            nc.scalar.activation(to, src, ACT.Identity).then_inc(thi, 1)
                        else:
                            for c in range(C):
                                ins = nc.scalar.activation(to[:, c, :], src[:, c, :], ACT.Identity, bias=bias_of(c))
                            ins.then_inc(thi, 1)

                    expo(0)
                    for b in range(B):
                        for k in range(HPC):
                            highs(b, k)
                        if b + 1 < B:
                            expo(b + 1)
                        highs(b, HPC)

        ph = ExitStack()
        cos, sin, rot = sb("cos", [P, T], F32, ph), sb("sin", [P, T], F32, ph), sb("rot", [P, P], F32, ph)
        causal = sb("causal", [T, C * T], FR, ph)
        wo = pair("l0_wo", [P, C, D], ph)
        qf, kf = sb("q_roped", [P, C, N], F32, ph), sb("k_roped", [P, C, N], F32, ph)
        v = pair("l0_v", [T, B, NH, VW], ph)
        wst = ExitStack()
        raw, (wq, wk, wv) = load_turned("l0w", ["Wq", "Wk", "Wv"], wst, wst)
        causal_f = sb("causal_f", [T, C * T], F32, wst)
        loads = [(cos[:], g["cos"]), (sin[:], g["sin"]), (rot[:], g["rot"]), (causal_f[:], g["causal"])]
        for r_, key in zip(raw, ("L0_attn_Wq", "L0_attn_Wk", "L0_attn_Wv")):
            loads.append((r_[:], natural(g[key])))
        load_stage("ld_l0", loads)
        ones_set = sem("ones_set")
        with nc.Block() as block:
            @block.vector
            def _(dve):
                nc.vector.tensor_copy(causal[:], causal_f[:]).then_inc(ones_set, 1)
                nc.vector.memset(v.hi[:, :, :, HD:HD + 1].bitcast(F32), 1.0).then_inc(ones_set, 1)
                nc.vector.memset(v.hi[:, :, :, HD + 1:].bitcast(F32), 0.0).then_inc(ones_set, 1)
                nc.vector.memset(v.lo[:, :, :, HD:].bitcast(F32), 0.0).then_inc(ones_set, 1)
        product_stage("turn_w0", turn_weight(raw[0], wq) + turn_weight(raw[1], wk) + turn_weight(raw[2], wv))
        load_stage("ld_wo0", [(raw[0][:], natural(g["L0_attn_Wo"]))])

        def value_jobs(srcT, w, dst, kc=C):
            res = []
            for b in range(B):
                products = []
                for k in range(kc):
                    products += times(srcT[:, k, b * T:(b + 1) * T], w[:, k, :])

                def emit(pe, bank, products=products):
                    return emit_products(pe, bank.rearrange("q h d -> q (h d)"), products)
                res.append((emit, lambda bank: bank[0:T, :].rearrange("q (h d) -> q h d", h=NH),
                            dst[:, b, :, 0:HD], None, 1.0))
            return res

        brow = lambda key, extra=0: (lambda m: BT[:, m, ROWS[key] + extra:ROWS[key] + extra + 1])
        product_stage("qkv0", turn_weight(raw[0], wo) + value_jobs(xT, wv, v)
                      + project(wq, xT, Pair(qf, qf), brow("L0_attn_bq"))[:0])

        def rope_stage():
            made, biased, swapped, t1s, t2s, done = (sem("rope_" + s) for s in
                                                     ("made", "biased", "swapped", "t1", "t2", "done"))
            t1, t2 = sb("rope_t1", [P, 2, HALF], F32, wst), sb("rope_t2", [P, 2, HALF], F32, wst)
            jobs = [(w, m, h, f, bkey) for w, f, bkey in ((wq, qf, "L0_attn_bq"), (wk, kf, "L0_attn_bk"))
                    for m in range(C) for h in range(2)]
            table = lambda t: t[:, :].unsqueeze(1).to_broadcast([P, HALF // T, T])
            by_batch = lambda a: a.rearrange("p (b t) -> p b t", t=T)
            with nc.Block() as block:
                @block.tensor
                def _(pe):
                    def swap(n):
                        w, m, h, f, bkey = jobs[n]
                        pe.wait_ge(biased, n + 1)
                        if n >= 4:
                            pe.wait_ge(t2s, n - 3)
                        nc.tensor.matmul(ps[:, 4 + n % 4, 0:HALF], rot[:, :], f[:, m, h * HALF:(h + 1) * HALF],
                                         start=True, stop=True).then_inc(swapped, 1)
                    for n, (w, m, h, f, bkey) in enumerate(jobs):
                        if n >= 4:
                            pe.wait_ge(biased, n - 3)
                        products = []
                        for k in range(C):
                            products += times(w[:, k, m * P:(m + 1) * P], xT[:, k, h * HALF:(h + 1) * HALF])
                        emit_products(nc.tensor, ps[:, n % 4, 0:HALF], products).then_inc(made, 1)
                        if n >= 1:
                            swap(n - 1)
                    swap(len(jobs) - 1)

                @block.scalar
                def _(act):
                    for n, (w, m, h, f, bkey) in enumerate(jobs):
                        act.wait_ge(made, n + 1)
                        nc.scalar.activation(f[:, m, h * HALF:(h + 1) * HALF], ps[:, n % 4, 0:HALF], ACT.Identity,
                                             bias=brow(bkey)(m)).then_inc(biased, 1)

                @block.gpsimd
                def _(pool):
                    for n, (w, m, h, f, bkey) in enumerate(jobs):
                        pool.wait_ge(biased, n + 1)
                        if n >= 2:
                            pool.wait_ge(done, n - 1)
                        nc.gpsimd.tensor_tensor(by_batch(t1[:, n % 2, :]), by_batch(f[:, m, h * HALF:(h + 1) * HALF]),
                                                table(cos), ALU.mult).then_inc(t1s, 1)

                @block.vector
                def _(dve):
                    for n, (w, m, h, f, bkey) in enumerate(jobs):
                        dve.wait_ge(swapped, n + 1)
                        if n >= 2:
                            dve.wait_ge(done, n - 1)
                        nc.vector.tensor_tensor(by_batch(t2[:, n % 2, :]), by_batch(ps[:, 4 + n % 4, 0:HALF]),
                                                table(sin), ALU.mult).then_inc(t2s, 1)
                        dve.wait_ge(t2s, n + 1)
                        dve.wait_ge(t1s, n + 1)
                        nc.vector.tensor_tensor(f[:, m, h * HALF:(h + 1) * HALF], t1[:, n % 2, :], t2[:, n % 2, :],
                                                ALU.add).then_inc(done, 1)
        rope_stage()
        wst.close()
        yT = xT
        att = ExitStack()
        bias_of = brow("L0_attn_bv")
        attention_stage("att0", qf, kf, v, yT, float(HD) ** -0.5, True, None, att)
        att.close()
        add_rows_stage("bo0")
        norm_stage("norm0", lambda pe, bank, b: emit_products(pe, bank, [
            p for k in range(C) for p in times(yT[:, k, b * T:(b + 1) * T], wo[:, k, :])]), x)
        ph.close()
        dump("d0")
        free_semaphores()

        def context_stage(name, qT, aT_out, queries_share, phase, scale, rowsum=None, qbk=None):
            raw = sb(name + "_ctx", [P, 2, KT, D], F32, phase)
            cn = pair(name + "_cn", [P, KT, D], phase)
            ct = pair(name + "_ct", [P, C, S], phase)
            pr = sb(name + "_p", [T, S], F32, phase) if not queries_share else sb(name + "_p", [P, KT, T], F32, phase)
            pT = pair(name + "_pT", [P, KT, T], phase)
            a = sb(name + "_a", [T, D], F32, phase)
            st = sb(name + "_st", [P, 4, 8], F32, phase)
            ld = [sem(f"{name}_landed{i}") for i in range(2)]
            (nhi, nlo, tp, thi, tlo, sc, red, ex, wt, whi, wlo, av, an, at, ahi, alo, ng) = (
                sem(f"{name}_{s}") for s in ("nhi", "nlo", "tp", "thi", "tlo", "sc", "red", "ex", "wt",
                                             "whi", "wlo", "av", "an", "at", "ahi", "alo", "ng"))
            whole = (KT - 1) * P
            keys = lambda j: P if j < KT - 1 else LAST
            pad = sem(name + "_pad")
            parts = [(0, 4, 512), (4, KT, S - 512)]
            with nc.Block() as block:
                @block.sync
                def _(sp):
                    for b in range(B):
                        if b >= 2:
                            sp.wait_ge(tp, 8 * (b - 1))
                            sp.wait_ge(nlo, b - 1)
                        sp.dma_start(raw[:, b % 2, 0:KT - 1, :],
                                     g["ctx_1024"][b, 0:whole, :].rearrange("(j p) d -> p j d", p=P)
                                     ).then_inc(ld[b % 2], 16)
                        sp.dma_start(raw[0:LAST, b % 2, KT - 1, :], g["ctx_1024"][b, whole:S, :]).then_inc(ld[b % 2], 16)

                @block.tensor
                def _(pe):
                    def turn(b):
                        pe.wait_ge(ld[b % 2], 32 * (b // 2 + 1))
                        for c in range(C):
                            for i, (j0, j1, w) in enumerate(parts):
                                n = 8 * b + 2 * c + i
                                if n >= 2:
                                    pe.wait_ge(tlo, n - 1)
                                for j in range(j0, j1):
                                    mm = nc.tensor.transpose(
                                        ps[:, n % 2, (j - j0) * P:(j - j0) * P + keys(j)],
                                        raw[0:keys(j), b % 2, j, c * P:(c + 1) * P], ident[0:keys(j), 0:keys(j)])
                                mm.then_inc(tp, 1)

                    def scores(b):
                        pe.wait_ge(tlo, 8 * (b + 1))
                        if b >= 1:
                            pe.wait_ge(ex, (1 if not queries_share else 2) * b)
                        q = qT[:, :, b * T:(b + 1) * T]
                        if not queries_share:
                            for i, (j0, j1, w) in enumerate(parts):
                                mm = emit_products(nc.tensor, ps[0:T, 2 + i, 0:w], [
                                    p for k in range(C) for p in times(q[:, k, :], ct[:, k, j0 * P:j0 * P + w])])
                        else:
                            for j in range(KT):
                                o = ps[0:keys(j), 2 + j // 5, j % 5 * T:(j % 5 + 1) * T]
                                products = [p for k in range(C) for p in times(
                                    ct[:, k, j * P:j * P + keys(j)], q[:, k, :])]
                                bias = [(ones_row[0:1, 0:keys(j)], qbk.hi[0:1, b * T:(b + 1) * T]),
                                        (ones_row[0:1, 0:keys(j)], qbk.lo[0:1, b * T:(b + 1) * T])]
                                mm = emit_products(nc.tensor, o, products + bias)
                        mm.then_inc(sc, 1)

                    def turn_p(b):
                        pe.wait_ge(ex, b + 1)
                        for i in range(2):
                            n = 2 * b + i
                            if n >= 2:
                                pe.wait_ge(wlo, n - 1)
                            for j in range(5 * i, min(KT, 5 * i + 5)):
                                mm = nc.tensor.transpose(ps[0:keys(j), 4 + i, j % 5 * T:(j % 5 + 1) * T],
                                                         pr[:, j * P:j * P + keys(j)], ident[0:T, 0:T])
                            mm.then_inc(wt, 1)

                    def values(b):
                        pe.wait_ge(wlo, 2 * (b + 1))
                        pe.wait_ge(nlo, b + 1)
                        if b >= 1:
                            pe.wait_ge(an, b)
                        mm = emit_products(nc.tensor, ps[0:T, 6, :], [
                            p for j in range(KT) for p in times(pT[0:keys(j), j, :], cn[0:keys(j), j, :])])
                        if rowsum is not None:
                            mm = emit_products(nc.tensor, ps[0:T, 7, C * T:C * T + 2], [
                                p for j in range(KT) for p in ((pT.hi[0:keys(j), j, :], ones_col[0:keys(j), :]),
                                                               (pT.lo[0:keys(j), j, :], ones_col[0:keys(j), :]))])
                        mm.then_inc(av, 1)

                    def turn_a(b):
                        pe.wait_ge(an, b + 1)
                        if b >= 1:
                            pe.wait_ge(alo, b)
                        for c in range(C):
                            mm = nc.tensor.transpose(ps[:, 7, c * T:(c + 1) * T], a[:, c * P:(c + 1) * P],
                                                     ident[0:T, 0:T])
                        mm.then_inc(at, 1)

                    turn(0)
                    for b in range(B):
                        scores(b)
                        if b + 1 < B:
                            pe.wait_ge(sc, b + 1)
                            turn(b + 1)
                        if not queries_share:
                            turn_p(b)
                        values(b)
                        turn_a(b)

                @block.scalar
                def _(act):
                    def highs(b):
                        for n in range(8 * b, 8 * b + 8):
                            c, i = n % 8 // 2, n % 2
                            j0, j1, w = parts[i]
                            act.wait_ge(tp, n + 1)
                            if b >= 1 and n % 8 == 0:
                                act.wait_ge(sc, b)
                            nc.scalar.activation(ct.hi[:, c, j0 * P:j0 * P + w], ps[:, n % 2, 0:w],
                                                 ACT.Identity).then_inc(thi, 1)

                    def soft(b):
                        if not queries_share:
                            act.wait_ge(ng, b + 1)
                            if b >= 1:
                                act.wait_ge(wt, 2 * b)
                            nc.scalar.activation(pr[:, :], ps[0:T, 2:4, :].rearrange("q i k -> q (i k)")[:, 0:S],
                                                 ACT.Exp, bias=st[0:T, 1, 0:1], scale=scale,
                                                 accum_out=st[0:T, 2, 0:1]).then_inc(ex, 1)
                        else:
                            act.wait_ge(ng, 2 * b + 2)
                            for i, (rw, j0, j1) in enumerate(((P, 0, KT - 1), (LAST, KT - 1, KT))):
                                nc.scalar.activation(pr[0:rw, j0:j1, :], pr[0:rw, j0:j1, :], ACT.Exp,
                                                     scale=scale).then_inc(whi if False else wt, 1)

                    def weights(b):
                        for i, (rw, j0, j1) in enumerate(((P, 0, KT - 1), (LAST, KT - 1, KT))):
                            n = 2 * b + i
                            if not queries_share:
                                act.wait_ge(wt, n + 1)
                                src = ps[0:rw, 4 + i, 0:(j1 - j0) * T].rearrange("p (j t) -> p j t", t=T)
                            else:
                                act.wait_ge(red, 8 * b + 7 + i)
                                src = pr[0:rw, j0:j1, :]
                            if b >= 1:
                                act.wait_ge(av, b)
                            nc.scalar.activation(pT.hi[0:rw, j0:j1, :], src, ACT.Identity).then_inc(whi, 1)

                    def out_high(b):
                        act.wait_ge(at, b + 1)
                        nc.scalar.activation(aT_out.hi[:, :, b * T:(b + 1) * T],
                                             ps[:, 7, 0:C * T].rearrange("p (c t) -> p c t", c=C),
                                             ACT.Identity).then_inc(ahi, 1)

                    highs(0)
                    for b in range(B):
                        soft(b)
                        if b + 1 < B and not queries_share:
                            pass
                        weights(b) if queries_share else None
                        if b + 1 < B:
                            highs(b + 1)
                        if not queries_share:
                            weights(b)
                        out_high(b)

                @block.gpsimd
                def _(pool):
                    for b in range(B):
                        pool.wait_ge(ld[b % 2], 32 * (b // 2 + 1))
                        if b >= 1:
                            pool.wait_ge(av, b)
                        nc.gpsimd.tensor_copy(cn.hi[:, 0:KT - 1, :], raw[:, b % 2, 0:KT - 1, :]).then_inc(nhi, 1)
                        nc.gpsimd.tensor_copy(cn.hi[0:LAST, KT - 1, :], raw[0:LAST, b % 2, KT - 1, :]).then_inc(nhi, 1)
                        pool.wait_ge(nhi, 2 * b + 2)
                        nc.gpsimd.tensor_tensor(cn.lo[:, 0:KT - 1, :], raw[:, b % 2, 0:KT - 1, :],
                                                cn.hi[:, 0:KT - 1, :].bitcast(F32), ALU.subtract).then_inc(pad, 1)
                        nc.gpsimd.tensor_tensor(cn.lo[0:LAST, KT - 1, :], raw[0:LAST, b % 2, KT - 1, :],
                                                cn.hi[0:LAST, KT - 1, :].bitcast(F32), ALU.subtract).then_inc(pad, 1)
                        pool.wait_ge(pad, 2 * b + 2)
                        pool.sem_inc(nlo, 1)

                @block.vector
                def _(dve):
                    def lows(b):
                        for n in range(8 * b, 8 * b + 8):
                            c, i = n % 8 // 2, n % 2
                            j0, j1, w = parts[i]
                            dve.wait_ge(thi, n + 1)
                            nc.vector.tensor_tensor(ct.lo[:, c, j0 * P:j0 * P + w], ps[:, n % 2, 0:w],
                                                    ct.hi[:, c, j0 * P:j0 * P + w].bitcast(F32),
                                                    ALU.subtract).then_inc(tlo, 1)

                    def soft(b):
                        dve.wait_ge(sc, b + 1)
                        if not queries_share:
                            if b >= 1:
                                dve.wait_ge(ex, b)
                            nc.vector.tensor_reduce(st[0:T, 0, 0:1], ps[0:T, 2:4, :].rearrange("q i k -> q (i k)")[:, 0:S],
                                                    AX.X, ALU.max).then_inc(red, 1)
                            dve.wait_ge(red, b + 1)
                            nc.vector.tensor_scalar(st[0:T, 1, 0:1], st[0:T, 0, 0:1], -scale, None,
                                                    ALU.mult).then_inc(ng, 1)
                            return
                        groups = ((P, 0, KT - 1), (LAST, KT - 1, KT))
                        if b >= 1:
                            dve.wait_ge(wlo, 2 * b)
                        for i, (rw, j0, j1) in enumerate(groups):
                            src = ps[0:rw, 2 + i, 0:(j1 - j0) * T].rearrange("p (j t) -> p j t", t=T)
                            nc.vector.tensor_reduce(st[0:rw, 0, j0:j1], src, AX.X, ALU.max).then_inc(red, 1)
                        dve.wait_ge(red, 8 * b + 2)
                        for i, (rw, j0, j1) in enumerate(groups):
                            src = ps[0:rw, 2 + i, 0:(j1 - j0) * T].rearrange("p (j t) -> p j t", t=T)
                            nc.vector.tensor_tensor(pr[0:rw, j0:j1, :], src,
                                                    st[0:rw, 0, j0:j1].unsqueeze(2).to_broadcast([rw, j1 - j0, T]),
                                                    ALU.subtract).then_inc(ng, 1)
                            dve.wait_ge(ng, 2 * b + i + 1)
                            dve.sem_inc(ex, 1)
                        for i, (rw, j0, j1) in enumerate(groups):
                            dve.wait_ge(wt, 2 * b + i + 1)
                            nc.vector.tensor_reduce(st[0:rw, 2, j0:j1], pr[0:rw, j0:j1, :], AX.X,
                                                    ALU.add).then_inc(red, 1)
                        dve.wait_ge(red, 8 * b + 4)
                        for i, (rw, j0, j1) in enumerate(groups):
                            nc.vector.reciprocal(st[0:rw, 3, j0:j1], st[0:rw, 2, j0:j1]).then_inc(red, 1)
                        dve.wait_ge(red, 8 * b + 6)
                        for i, (rw, j0, j1) in enumerate(groups):
                            nc.vector.tensor_tensor(pr[0:rw, j0:j1, :], pr[0:rw, j0:j1, :],
                                                    st[0:rw, 3, j0:j1].unsqueeze(2).to_broadcast([rw, j1 - j0, T]),
                                                    ALU.mult).then_inc(red, 1)

                    def weights(b):
                        for i, (rw, j0, j1) in enumerate(((P, 0, KT - 1), (LAST, KT - 1, KT))):
                            dve.wait_ge(whi, 2 * b + i + 1)
                            src = (pr[0:rw, j0:j1, :] if queries_share else
                                   ps[0:rw, 4 + i, 0:(j1 - j0) * T].rearrange("p (j t) -> p j t", t=T))
                            nc.vector.tensor_tensor(pT.lo[0:rw, j0:j1, :], src, pT.hi[0:rw, j0:j1, :].bitcast(F32),
                                                    ALU.subtract).then_inc(wlo, 1)

                    def outputs(b):
                        dve.wait_ge(av, b + 1)
                        if b >= 1:
                            dve.wait_ge(at, b)
                        if not queries_share:
                            nc.vector.reciprocal(st[0:T, 3, 0:1], st[0:T, 2, 0:1]).then_inc(nhi2, 1)
                            dve.wait_ge(nhi2, b + 1)
                            nc.vector.tensor_scalar(a[:, :], ps[0:T, 6, :], st[0:T, 3, 0:1], None,
                                                    ALU.mult).then_inc(an, 1)
                        else:
                            nc.vector.tensor_copy(rowsum[:, b:b + 1], ps[0:T, 7, C * T:C * T + 1]).then_inc(nhi2, 1)
                            dve.wait_ge(nhi2, b + 1)
                            nc.vector.tensor_copy(a[:, :], ps[0:T, 6, :]).then_inc(an, 1)
                        dve.wait_ge(ahi, b + 1)
                        nc.vector.tensor_tensor(aT_out.lo[:, :, b * T:(b + 1) * T],
                                                ps[:, 7, 0:C * T].rearrange("p (c t) -> p c t", c=C),
                                                aT_out.hi[:, :, b * T:(b + 1) * T].bitcast(F32),
                                                ALU.subtract).then_inc(alo, 1)

                    nhi2 = sem(name + "_rc")
                    lows(0)
                    for b in range(B):
                        soft(b)
                        if queries_share:
                            weights(b)
                        if b + 1 < B:
                            lows(b + 1)
                        if not queries_share:
                            weights(b)
                        outputs(b)

        ph = ExitStack()
        wv = pair("x0_wv", [P, C, D], ph)
        qT = pair("x0_qT", [P, C, N], ph)
        st1 = ExitStack()
        m0 = pair("x0_m", [P, C, D], st1)
        rq, rk, rv = (sb(f"x0_raw{i}", [P, C, D], F32, st1) for i in range(3))
        pq, pk = pair("x0_pq", [P, C, D], st1), pair("x0_pk", [P, C, D], st1)
        load_stage("ld_x0", [(rq[:], natural(g["L0_xattn_WQ"])), (rk[:], natural(g["L0_xattn_WK"])),
                             (rv[:], natural(g["L0_xattn_WV"]))])
        split_stage("split_x0", [(pq[:, :, :], rq[:]), (pk[:, :, :], rk[:])])
        product_stage("m0", [tile_job([p for k in range(C) for p in times(pq[:, k, m * P:(m + 1) * P], pk[:, k, :])],
                                      m0[:, m, :], cols=D) for m in range(C)] + turn_weight(rv, wv))
        product_stage("q0", project(m0, xT, qT))
        st1.close()
        yT = xT
        st2 = ExitStack()
        context_stage("ctx0", qT, yT, False, st2, float(D) ** -0.5)
        st2.close()
        norm_stage("norm1", lambda pe, bank, b: emit_products(pe, bank, [
            p for k in range(C) for p in times(yT[:, k, b * T:(b + 1) * T], wv[:, k, :])]), x)
        ph.close()
        dump("d1")
        free_semaphores()

        ph = ExitStack()
        indT = sb("indT", [E, N], FR, ph)
        w_dram = nc.dram_tensor("token_weights", [E, N], F32).ap()
        gt = ExitStack()
        gw = sb("gate_w", [P, C, E], F32, gt)
        gb = sb("gate_b", [E, 1], F32, gt)
        iota8 = sb("iota8", [P, E], F32, gt)
        xf = sb("xf", [P, C, HALF], F32, gt)
        lg = sb("logits", [E, B, T], F32, gt)
        gs = sb("gate_stat", [E, 3, B], F32, gt)
        prn = sb("probs", [T, B, E], F32, gt)
        m8 = sb("top8", [T, B, E], F32, gt)
        i8 = sb("top8_index", [T, B, E], U32, gt)
        i8f = sb("top8_index_f", [T, B, E], F32, gt)
        ind = sb("chosen", [T, B, E], F32, gt)
        ind2 = sb("chosen2", [T, B, E], F32, gt)
        wn = sb("token_w", [T, B, E], F32, gt)
        wT = sb("token_wT", [E, N], F32, gt)
        load_stage("ld_gate", [(gw[:], g["L0_ffn_gate_w"].rearrange("(c p) e -> p c e", p=P)),
                               (gb[:], g["L0_ffn_gate_b"].unsqueeze(1)), (iota8[:], g["iota8"])])
        chain, mm_s, lg_s, stored = sem("gate_chain"), sem("gate_mm"), sem("gate_act"), sem("gate_stored")
        with nc.Block() as block:
            CH = {}

            @block.vector
            def _(dve):
                count = [0]

                def step(ins):
                    ins.then_inc(chain, 1)
                    count[0] += 1
                    dve.wait_ge(chain, count[0])
                for h in range(2):
                    if h == 1:
                        dve.wait_ge(mm_s, 1)
                    step(nc.vector.tensor_tensor(xf[:], xT.hi[:, :, h * HALF:(h + 1) * HALF].bitcast(F32),
                                                 xT.lo[:, :, h * HALF:(h + 1) * HALF].bitcast(F32), ALU.add))
                dve.wait_ge(lg_s, 2)
                step(nc.vector.tensor_reduce(gs[:, 0, :], lg[:], AX.X, ALU.max))
                step(nc.vector.tensor_tensor(lg[:], lg[:], gs[:, 0, :].unsqueeze(2).to_broadcast([E, B, T]),
                                             ALU.subtract))
                CH["sub"] = count[0]
                dve.wait_ge(lg_s, 3)
                step(nc.vector.tensor_reduce(gs[:, 1, :], lg[:], AX.X, ALU.add))
                step(nc.vector.reciprocal(gs[:, 2, :], gs[:, 1, :]))
                step(nc.vector.tensor_tensor(lg[:], lg[:], gs[:, 2, :].unsqueeze(2).to_broadcast([E, B, T]),
                                             ALU.mult))
                CH["probs"] = count[0]
                dve.wait_ge(mm_s, 3)
                step(nc.vector.tensor_copy(prn[:].rearrange("t b e -> t (b e)"), ps[0:T, 2, 0:B * E]))
                for b in range(B):
                    step(nc.vector.max(m8[:, b, :], prn[:, b, :]))
                    step(nc.vector.max_index(i8[:, b, :], m8[:, b, :], prn[:, b, :]))
                step(nc.vector.tensor_copy(i8f[:], i8[:]))
                io = iota8[0:T, :].unsqueeze(1).to_broadcast([T, B, E])
                step(nc.vector.tensor_tensor(ind[:], io, i8f[:, :, 0:1].to_broadcast([T, B, E]), ALU.is_equal))
                step(nc.vector.tensor_tensor(ind2[:], io, i8f[:, :, 1:2].to_broadcast([T, B, E]), ALU.is_equal))
                step(nc.vector.tensor_tensor(ind[:], ind[:], ind2[:], ALU.add))
                step(nc.vector.tensor_tensor(wn[:], ind[:], prn[:], ALU.mult))
                CH["chosen"] = count[0]
                dve.wait_ge(mm_s, 4)
                for h in range(2):
                    step(nc.vector.tensor_copy(indT[:, h * HALF:(h + 1) * HALF], ps[0:E, 3 + h, 0:HALF]))
                for h in range(2):
                    step(nc.vector.tensor_copy(wT[:, h * HALF:(h + 1) * HALF], ps[0:E, 5 + h, 0:HALF]))
                CH["wT"] = count[0]

            @block.tensor
            def _(pe):
                for h in range(2):
                    pe.wait_ge(chain, h + 1)
                    mm = emit_products(nc.tensor, ps[0:E, h, 0:HALF], [(gw[:, k, :], xf[:, k, :]) for k in range(C)])
                    mm.then_inc(mm_s, 1)
                pe.wait_ge(chain, CH["probs"])
                for b in range(B):
                    mm = nc.tensor.transpose(ps[0:T, 2, b * E:(b + 1) * E], lg[:, b, :], ident[0:E, 0:E])
                mm.then_inc(mm_s, 1)
                pe.wait_ge(chain, CH["chosen"])
                for b in range(B):
                    nc.tensor.transpose(ps[0:E, 3 + b // 4, b % 4 * T:(b % 4 + 1) * T], ind[:, b, :], ident[0:T, 0:T])
                    mm = nc.tensor.transpose(ps[0:E, 5 + b // 4, b % 4 * T:(b % 4 + 1) * T], wn[:, b, :], ident[0:T, 0:T])
                mm.then_inc(mm_s, 1)

            @block.scalar
            def _(act):
                for h in range(2):
                    act.wait_ge(mm_s, h + 1)
                    nc.scalar.activation(lg[:, 4 * h:4 * h + 4, :].rearrange("e b t -> e (b t)"), ps[0:E, h, 0:HALF],
                                         ACT.Identity, bias=gb[:]).then_inc(lg_s, 1)
                act.wait_ge(chain, CH["sub"])
                nc.scalar.activation(lg[:], lg[:], ACT.Exp).then_inc(lg_s, 1)

            @block.sync
            def _(sp):
                sp.wait_ge(chain, CH["wT"])
                sp.dma_start(w_dram, wT[:]).then_inc(stored, 16)
                sp.wait_ge(stored, 16)
        gt.close()

        hA, hB = pair("hA", [P, C, N], ph), pair("hB", [P, C, N], ph)
        V = sb("v_turned", [P, C, E], F32, ph)
        Vn = pair("v_natural", [E, D], ph)

        ff = ExitStack()
        wraw = sb("ffn_raw", [P, 2, C, D], F32, ff)
        w = pair("ffn_w", [P, 2, C, D], ff)
        hf = sb("ffn_h", [P, 4, HALF], F32, ff)
        wb = sb("ffn_wb", [P, 2, N], F32, ff)
        part = sb("ffn_part", [P, 2, C, 2], F32, ff)
        (fwh, fwl, fmm, frelu, fhi, flo, fred, fsum) = (sem("ffn_" + s) for s in (
            "w_hi", "w_lo", "made", "relu", "h_hi", "h_lo", "reduced", "summed"))
        fprod, fbias = sem("ffn_product"), sem("ffn_bias")
        fl = [sem(f"ffn_landed{i}") for i in range(2)]
        fwb = [sem(f"ffn_wb_landed{i}") for i in range(2)]
        bslot = sb("ffn_bias_now", [P, 6, C], F32, ff)
        LPI = 6
        TPL = 2 * C
        expert_w = [g[f"L0_ffn_w{i}"].rearrange("e (c p) o -> e p c o", p=P) for i in (1, 2, 3)]
        srcs = [xT, hA, hB]
        LPE = 3
        HPL = 2 * (LPE - 1) * TPL
        TPR = LPI * TPL
        MADE0 = TPL + 1
        with nc.Block() as block:
            @block.sync
            def _(sp):
                for l in range(2):
                    sp.dma_start(wraw[:, l, :, :], expert_w[l][0]).then_inc(fl[l], 16)
                with sp.Fori(0, E // 2) as j:
                    sp.wait_ge(fsum, 2 * j + 1)
                    for e2 in range(2):
                        sp.dma_start(wb[:, e2, :], w_dram[bass.ds(2 * j + e2, 1), :].to_broadcast([P, N])
                                     ).then_inc(fwb[e2], 16)
                    for l in range(LPI):
                        sp.wait_ge(fwl, LPI * j + l + 1)
                        ahead = l + 2
                        sp.dma_start(wraw[:, l % 2, :, :],
                                     expert_w[ahead % LPE][bass.ds((2 * j + ahead // LPE) % E, 1)]
                                     .rearrange("a p c o -> p (a c) o")).then_inc(fl[l % 2], 16)
                for l in range(2):
                    sp.wait_ge(fl[l], 16 * (LPE * E // 2 + 1))

            @block.tensor
            def _(pe):
                pe.sem_inc(fmm, MADE0)
                with pe.Fori(0, E // 2) as j:
                    for l in range(LPI):
                        pe.wait_ge(fwl, LPI * j + l + 1)
                        src = srcs[l % LPE]
                        for n in range(TPL):
                            m, h = n // 2, n % 2
                            t = TPL * l + n
                            pe.wait_ge(frelu, TPR * j + t + 1)
                            if l % LPE and n < 2:
                                pe.wait_ge(flo, HPL * j + TPL * ((LPE - 1) * (l // LPE) + l % LPE) - 1 + n)
                            emit_products(nc.tensor, ps[:, t % 8, 0:HALF], [
                                p for k in range(C) for p in times(w[:, l % 2, k, m * P:(m + 1) * P],
                                                                   src[:, k, h * HALF:(h + 1) * HALF])
                            ]).then_inc(fmm, 1)

            @block.scalar
            def _(act):
                def split(j, l):
                    act.wait_ge(fl[l % 2], 16 * (LPI // 2 * j + l // 2 + 1))
                    act.wait_ge(fmm, MADE0 + TPR * j + TPL * (l - 1))
                    nc.scalar.activation(w.hi[:, l % 2, :, :], wraw[:, l % 2, :, :], ACT.Identity).then_inc(fwh, 1)

                act.sem_inc(frelu, 8)
                split(0, 0)
                with act.Fori(0, E // 2) as j:
                    for l in range(LPI):
                        nc.scalar.activation(
                            bslot[:, l, :].unsqueeze(2),
                            BT[:, :, bass.ds(2 * j + (ROWS[f"L0_ffn_b{l % LPE + 1}"] + l // LPE), 1)],
                            ACT.Identity).then_inc(fbias, 1)
                        act.wait_ge(fbias, LPI * j + l + 1)
                        for n in range(TPL):
                            t = TPL * l + n
                            m = n // 2
                            act.wait_ge(fmm, MADE0 + TPR * j + t + 1)
                            act.wait_ge(fhi, TPR * j + t + 1)
                            nc.scalar.activation(hf[:, t % 4, :], ps[:, t % 8, 0:HALF], ACT.Relu,
                                                 bias=bslot[:, l, m:m + 1]).then_inc(frelu, 1)
                            if n == 2:
                                split(j, l + 1)

            @block.vector
            def _(dve):
                def split(j, l):
                    dve.wait_ge(fwh, LPI * j + l + 1)
                    nc.vector.tensor_tensor(w.lo[:, l % 2, :, :], wraw[:, l % 2, :, :],
                                            w.hi[:, l % 2, :, :].bitcast(F32), ALU.subtract).then_inc(fwl, 1)

                dve.sem_inc(fhi, 4)
                dve.sem_inc(fsum, 1)
                split(0, 0)
                with dve.Fori(0, E // 2) as j:
                    for l in range(LPI):
                        for n in range(TPL):
                            t = TPL * l + n
                            m, h = n // 2, n % 2
                            dve.wait_ge(frelu, TPR * j + t + 1 + 8)
                            if l % LPE < LPE - 1:
                                dst = (hA, hB)[l % LPE][:, m, h * HALF:(h + 1) * HALF]
                                k = TPL * ((LPE - 1) * (l // LPE) + l % LPE) + n
                                nc.vector.tensor_copy(dst.hi, hf[:, t % 4, :]).then_inc(fred, 1)
                                dve.wait_ge(fred, HPL * j + k + 1)
                                nc.vector.tensor_tensor(dst.lo, hf[:, t % 4, :], dst.hi.bitcast(F32),
                                                        ALU.subtract).then_inc(flo, 1)
                                dve.wait_ge(flo, HPL * j + k + 1)
                            else:
                                e2 = l // LPE
                                k = TPL * e2 + n
                                if n == 0:
                                    dve.wait_ge(fwb[e2], 16 * (j + 1))
                                nc.vector.tensor_tensor_reduce(
                                    out=hf[:, t % 4, :], in0=hf[:, t % 4, :], in1=wb[:, e2, h * HALF:(h + 1) * HALF],
                                    scale=1.0, scalar=0.0, op0=ALU.mult, op1=ALU.add,
                                    accum_out=part[:, e2, m, h:h + 1]).then_inc(fprod, 1)
                                dve.wait_ge(fprod, 2 * TPL * j + k + 1)
                            dve.sem_inc(fhi, 1)
                            if n == 2:
                                split(j, l + 1)
                        if l % LPE == LPE - 1:
                            e2 = l // LPE
                            nc.vector.tensor_tensor(V[:, :, bass.ds(2 * j + e2, 1)], part[:, e2, :, 0:1],
                                                    part[:, e2, :, 1:2], ALU.add).then_inc(fsum, 1)
        ff.close()
        product_stage("turn_v", [flip_job([(c * P, V[:, c, :]) for c in range(C)], Vn[:, :], rows=E, cols=D)])
        norm_stage("norm2", lambda pe, bank, b: emit_products(pe, bank, [
            (indT[:, b * T:(b + 1) * T], Vn.hi[:, :]), (indT[:, b * T:(b + 1) * T], Vn.lo[:, :])]), x)
        ph.close()
        dump("d2")
        free_semaphores()

        ph = ExitStack()
        wo = pair("l1_wo", [P, C, D], ph)
        qf, kf = sb("l1_q", [P, C, N], F32, ph), sb("l1_k", [P, C, N], F32, ph)
        v = pair("l1_v", [T, B, NH, VW], ph)
        decay = sb("decay", [T, T], F32, ph)
        st1 = ExitStack()
        rk, rv = sb("l1_rk", [P, C, D], F32, st1), sb("l1_rv", [P, C, D], F32, st1)
        rq = sb("l1_rq", [P, C, D], F32, st1)
        rd = sb("l1_rd", [P, C, LAT], F32, st1)
        ru, rw = sb("l1_ru", [P, D], F32, st1), sb("l1_rw", [P, D], F32, st1)
        load_stage("ld_l1a", [(rk[:], natural(g["L1_attn_Wk"])), (rv[:], natural(g["L1_attn_Wv"])),
                              (rd[:], g["L1_attn_W_down_kv"].rearrange("(c p) l -> p c l", p=P)),
                              (ru[:], g["L1_attn_W_up_k"]), (rw[:], g["L1_attn_W_up_v"]),
                              (rq[:], natural(g["L1_attn_Wq"])), (decay[:], g["decay"])])
        kv_sum = sem("kv_sum")
        with nc.Block() as block:
            @block.vector
            def _(dve):
                nc.vector.tensor_tensor(rk[:], rk[:], rv[:], ALU.add).then_inc(kv_sum, 1)
                nc.vector.memset(v.hi[:, :, :, HD:HD + 1].bitcast(F32), 1.0).then_inc(kv_sum, 1)
                nc.vector.memset(v.hi[:, :, :, HD + 1:].bitcast(F32), 0.0).then_inc(kv_sum, 1)
                nc.vector.memset(v.lo[:, :, :, HD:].bitcast(F32), 0.0).then_inc(kv_sum, 1)
        pd, wd = pair("l1_pd", [P, C, LAT], st1), pair("l1_wd", [P, C, LAT], st1)
        pu, pw = pair("l1_pu", [P, 1, D], st1), pair("l1_pw", [P, 1, D], st1)
        pq = pair("l1_pq", [P, C, D], st1)
        split_stage("split_l1", [(pd[:, :, :], rd[:]), (pu[:, 0, :], ru[:]), (pw[:, 0, :], rw[:]),
                                 (pq[:, :, :], rq[:])])
        sT = pair("l1_sT", [P, C, D], st1)
        latT = pair("l1_latT", [P, 1, N], st1)
        product_stage("turn_kv", turn_weight(rk, sT))
        load_stage("ld_wo1", [(rv[:], natural(g["L1_attn_Wo"]))])
        split_stage("split_wo1", [(wo[:, :, :], rv[:])])
        product_stage("down", [tile_job([p for k in range(C) for p in times(sT[:, k, m * P:(m + 1) * P], pd[:, k, :])],
                                        wd[:, m, :], cols=LAT) for m in range(C)])
        scale1 = float(1.0 / (np.sqrt(np.float32(D)) + np.float32(1e-8)))
        fjobs = lambda js, dst: [(e, vw, dst[:, n // 2, n % 2 * HALF:(n % 2 + 1) * HALF], bi, s)
                                 for n, (e, vw, d, bi, s) in enumerate(js)]
        product_stage("lat", project(wd, xT, latT, mc=1) + fjobs(project(pq, xT, xT, scale=scale1), qf))
        product_stage("up", fjobs(project(pu, latT, xT, kc=1), kf) + value_jobs(latT, pw, v, kc=1))
        st1.close()
        yT = xT
        att = ExitStack()
        bias_of = None
        attention_stage("att1", qf, kf, v, yT, 1.0, False, decay, att)
        att.close()
        norm_stage("norm3", lambda pe, bank, b: emit_products(pe, bank, [
            p for k in range(C) for p in times(yT[:, k, b * T:(b + 1) * T], wo[:, k, :])]), x)
        ph.close()
        dump("d3")
        free_semaphores()

        ph = ExitStack()
        n1 = pair("x1_n", [P, C, D], ph)
        qbk = pair("x1_qbk", [1, N], ph)
        bvo = sb("x1_bvo", [P, D], F32, ph)
        ones_row, ones_col = sb("ones_row", [1, P], FR, ph), sb("ones_col", [P, 2], FR, ph)
        rowsum = sb("rowsum", [T, B], F32, ph)
        aux = sb("x1_aux", [P, 2, C], F32, ph)
        bb = sb("x1_bb", [1, 2], F32, ph)
        col = lambda key, k: BT[:, k % C, ROWS[key] + k // C:ROWS[key] + k // C + 1]
        st2 = ExitStack()
        ra, rb = sb("x1_rv", [P, HC, D], F32, st2), sb("x1_ro", [P, C, HID], F32, st2)
        pv_, poT = pair("x1_pv", [P, HC, D], st2), pair("x1_poT", [P, HC, D], st2)
        bvb = pair("x1_bvb", [P, HC, P], st2)
        load_stage("ld_x1b", [(ra[:], hid(g["L1_xattn_Wv"])), (rb[:], natural(g["L1_xattn_Wo"]))])
        split_stage("split_x1b", [(pv_[:, :, :], ra[:])] + [
            (bvb[:, k, :], col("L1_xattn_bv", k).to_broadcast([P, P])) for k in range(HC)])
        product_stage("turn_wo", turn_weight(rb, poT, C, HC))
        product_stage("n1", [tile_job([p for k in range(HC) for p in times(pv_[:, k, m * P:(m + 1) * P], poT[:, k, :])],
                                      n1[:, m, :], cols=D) for m in range(C)]
                      + [tile_job([p for k in range(HC) for p in times(bvb[:, k, :], poT[:, k, :])],
                                  bvo[:, :], cols=D)])
        st2.close()
        m1 = pair("x1_m", [P, C, D], ph)
        uf = pair("x1_u", [P, C, P], ph)
        stA = ExitStack()
        ra, rb = sb("x1_ra", [P, HC, D], F32, stA), sb("x1_rb", [P, HC, D], F32, stA)
        pa, pb = pair("x1_pa", [P, HC, D], stA), pair("x1_pb", [P, HC, D], stA)
        load_stage("ld_x1a", [(ra[:], hid(g["L1_xattn_Wq"])), (rb[:], hid(g["L1_xattn_Wk"])),
                              (bo_rows[:], g["L1_xattn_bo"].partition_broadcast(P))])
        split_stage("split_x1", [(pa[:, :, :], ra[:]), (pb[:, :, :], rb[:])])
        ones = sem("ones1")
        onesf = sb("onesf", [P, P], F32, stA)
        with nc.Block() as block:
            @block.vector
            def _(dve):
                nc.vector.memset(onesf[:], 1.0).then_inc(ones, 1)
                dve.wait_ge(ones, 1)
                nc.vector.tensor_copy(ones_row[:], onesf[0:1, :]).then_inc(ones, 1)
                nc.vector.tensor_copy(ones_col[:], onesf[:, 0:2]).then_inc(ones, 1)
                nc.vector.memset(uf.hi[:].bitcast(F32), 0.0).then_inc(ones, 1)
                nc.vector.memset(uf.lo[:].bitcast(F32), 0.0).then_inc(ones, 1)

        def col_job(w_, key, m, dst):
            def emit(pe, bank):
                return emit_products(pe, bank, [(w_[:, k, m * P:(m + 1) * P], col(key, k)) for k in range(HC)])
            return (emit, lambda bank: bank[:, 0:1], dst, None, 1.0)
        jobs = [tile_job([p for k in range(HC) for p in times(pa[:, k, m * P:(m + 1) * P], pb[:, k, :])],
                         m1[:, m, :], cols=D) for m in range(C)]
        jobs += [col_job(rb, "L1_xattn_bq", m, aux[:, 0, m:m + 1]) for m in range(C)]
        jobs += [col_job(ra, "L1_xattn_bk", m, uf[:, m, 0:1]) for m in range(C)]
        jobs += [(lambda pe, bank: emit_products(pe, bank, [(col("L1_xattn_bq", k), col("L1_xattn_bk", k))
                                                            for k in range(HC)]),
                  lambda bank: bank[0:1, 0:1], bb[0:1, 0:1], None, 1.0)]
        product_stage("m1", jobs)
        stA.close()
        add_rows_stage("bo1")
        qb_jobs = [(lambda pe, bank, h=h: emit_products(pe, bank, [
            p for k in range(C) for p in times(uf[:, k, :], xT[:, k, h * HALF:(h + 1) * HALF])]),
            lambda bank: bank[:, 0:HALF], None, None, 1.0) for h in range(2)]

        def qbk_stage():
            made, hi_d, lo_d = sem("qbk_made"), sem("qbk_hi"), sem("qbk_lo")
            with nc.Block() as block:
                @block.tensor
                def _(pe):
                    for h in range(2):
                        qb_jobs[h][0](nc.tensor, ps[:, h, 0:HALF]).then_inc(made, 1)

                @block.scalar
                def _(act):
                    for h in range(2):
                        act.wait_ge(made, h + 1)
                        nc.scalar.activation(qbk.hi[0:1, h * HALF:(h + 1) * HALF], ps[0:1, h, 0:HALF],
                                             ACT.Identity, bias=bb[0:1, 0:1]).then_inc(hi_d, 1)

                @block.vector
                def _(dve):
                    for h in range(2):
                        dve.wait_ge(hi_d, h + 1)
                        nc.vector.scalar_tensor_tensor(qbk.lo[0:1, h * HALF:(h + 1) * HALF], ps[0:1, h, 0:HALF],
                                                       bb[0:1, 0:1], qbk.hi[0:1, h * HALF:(h + 1) * HALF].bitcast(F32),
                                                       ALU.add, ALU.subtract).then_inc(lo_d, 1)
        qbk_stage()
        qT = pair("x1_qT", [P, C, N], ph)
        product_stage("q1", project(m1, xT, qT, bias=lambda m: aux[:, 0, m:m + 1]))
        yT = xT
        st2 = ExitStack()
        context_stage("ctx1", qT, yT, True, st2, 64.0 ** -0.5, rowsum, qbk)
        st2.close()
        z = sb("x1_z", [T, 2, D], F32, ph)
        norm_stage("norm4", lambda pe, bank, b: emit_products(pe, bank, [
            p for k in range(C) for p in times(yT[:, k, b * T:(b + 1) * T], n1[:, k, :])]), x,
            gain=lambda b: (rowsum[:, b:b + 1], bvo[0:T, :]), turned=False, z=z)
        ph.close()
        dump("d4")
        free_semaphores()

        ph = ExitStack()
        kb16 = sb("k16", [P, C, D], BF16, ph)
        kq = sb("kq", [P, C, D], BF16, ph)
        sc_in, sc_k = sb("s_in", [P, 4], F32, ph), sb("s_k", [P, 4], F32, ph)
        bias16 = sb("bias16", [P, D], BF16, ph)
        identB = sb("identB", [P, P], BF16, ph)
        x16 = sb("x16", [T, B, D], BF16, ph)
        xq = sb("xq", [T, B, D], BF16, ph)
        xqT = sb("xqT", [P, C, N], BF16, ph)
        y16 = sb("y16", [T, B, D], BF16, ph)
        sx = [sb(f"quant{i}", [P, 4 * D], F32, ph) for i in range(3)]
        load_stage("ld_f8", [(kb16[:], natural(g["L1_ffn_kernel"])), (bias16[:], g["L1_ffn_bias"].partition_broadcast(P)),
                             (sc_in[:, 0:1], g["L1_ffn_input_scale"].partition_broadcast(P)),
                             (sc_k[:, 0:1], g["L1_ffn_kernel_scale"].partition_broadcast(P))])
        qs, tps, cps, mms, evs, bss = (sem("f8_" + s) for s in ("step", "turned", "copied", "made", "scaled", "biased"))
        with nc.Block() as block:
            F8 = {}

            @block.vector
            def _(dve):
                count = [0]

                def step(ins):
                    ins.then_inc(qs, 1)
                    count[0] += 1
                    dve.wait_ge(qs, count[0])

                def quantise(dst, src, inv, rows_, n):
                    v_, m_, t_ = (s[0:rows_, 0:n] for s in sx)
                    step(nc.vector.tensor_scalar(v_, src, inv, None, ALU.mult))
                    step(nc.vector.tensor_scalar(m_.bitcast(I32), v_.bitcast(I32), 0x7F800000, None, ALU.bitwise_and))
                    step(nc.vector.tensor_scalar(m_, m_, 2.0 ** -6, 1.5 * 2.0 ** 20, ALU.max, ALU.mult))
                    step(nc.vector.tensor_tensor(v_, v_, m_, ALU.add))
                    step(nc.vector.tensor_tensor(v_, v_, m_, ALU.subtract))
                    step(nc.vector.tensor_scalar(t_.bitcast(I32), v_.bitcast(I32), 0x7FFFFFFF, None, ALU.bitwise_and))
                    step(nc.vector.tensor_scalar(t_, t_, 448.0, 3e38, ALU.is_gt, ALU.mult))
                    step(nc.vector.scalar_tensor_tensor(dst, t_, 3e38, v_, ALU.mult, ALU.add))

                step(nc.vector.tensor_copy(identB[:], ident[:]))
                step(nc.vector.reciprocal(sc_in[:, 1:2], sc_in[:, 0:1]))
                step(nc.vector.reciprocal(sc_k[:, 1:2], sc_k[:, 0:1]))
                step(nc.vector.tensor_tensor(sc_in[:, 2:3], sc_in[:, 0:1], sc_k[:, 0:1], ALU.mult))
                quantise(kq[:].rearrange("p c d -> p (c d)"), kb16[:].rearrange("p c d -> p (c d)"),
                         sc_k[:, 1:2], P, C * D)
                for h in range(2):
                    step(nc.vector.tensor_copy(x16[:, 4 * h:4 * h + 4, :], x[0:T, 4 * h:4 * h + 4, :]))
                    quantise(xq[:, 4 * h:4 * h + 4, :].rearrange("t b d -> t (b d)"),
                             x16[:, 4 * h:4 * h + 4, :].rearrange("t b d -> t (b d)"), sc_in[0:T, 1:2], T, 4 * D)
                    F8[h] = count[0]
                for b in range(B):
                    dve.wait_ge(evs, b + 1)
                    nc.vector.tensor_tensor(y16[:, b, :], y16[:, b, :], bias16[0:T, :], ALU.add).then_inc(bss, 1)

            @block.tensor
            def _(pe):
                for b in range(B):
                    pe.wait_ge(qs, F8[b // 4])
                    if b >= 2:
                        pe.wait_ge(cps, b - 1)
                    bank = ps[:, b % 2, :].bitcast(BF16)
                    for c in range(C):
                        mm = nc.tensor.transpose(bank[:, c * T:(c + 1) * T], xq[:, b, c * P:(c + 1) * P],
                                                 identB[0:T, 0:T])
                    mm.then_inc(tps, 1)
                    pe.wait_ge(cps, b + 1)
                    if b >= 4:
                        pe.wait_ge(evs, b - 3)
                    emit_products(nc.tensor, ps[0:T, 2 + b % 4, :], [(xqT[:, k, b * T:(b + 1) * T], kq[:, k, :])
                                                                     for k in range(C)]).then_inc(mms, 1)

            @block.scalar
            def _(act):
                for b in range(B):
                    act.wait_ge(tps, b + 1)
                    bank = ps[:, b % 2, :].bitcast(BF16)
                    nc.scalar.activation(xqT[:, :, b * T:(b + 1) * T],
                                         bank[:, 0:C * T].rearrange("p (c t) -> p c t", c=C),
                                         ACT.Identity).then_inc(cps, 1)
                    act.wait_ge(mms, b + 1)
                    nc.scalar.activation(y16[:, b, :], ps[0:T, 2 + b % 4, :], ACT.Identity,
                                         scale=sc_in[0:T, 2:3]).then_inc(evs, 1)
        y32 = sb("y32", [T, B, D], F32, ph)
        wide = sem("wide")
        with nc.Block() as block:
            @block.vector
            def _(dve):
                nc.vector.tensor_tensor(y32[:], x[0:T, :, :], y16[:], ALU.add).then_inc(wide, 1)
        norm_stage("norm5", lambda pe, bank, b: pe.matmul(bank, zero[0:1, 0:T], zero[0:1, 0:D], start=True, stop=True)
                   if False else emit_products(pe, bank, [(identR[0:T, 0:T], zeroR[0:T, :])]), y32, turned=False, last=True) \
            if False else final_norm(nc, sem, ps, x, y32, stats, mv, rstd, minus_half, out)
        ph.close()


def final_norm(nc, sem, ps, x, y, stats, mv, rstd, minus_half, out):
    stat, aggr, rooted, normed, stored = (sem("last_" + s) for s in ("stat", "aggr", "rooted", "normed", "stored"))
    with nc.Block() as block:
        @block.vector
        def _(dve):
            for b in range(B):
                nc.vector.bn_stats(stats[0:T, b, :], y[:, b, :]).then_inc(stat, 1)
                dve.wait_ge(stat, b + 1)
                nc.vector.bn_aggr(mv[0:T, b, :], stats[0:T, b, :]).then_inc(aggr, 1)
            for b in range(B):
                dve.wait_ge(rooted, 2)
                nc.vector.tensor_scalar(x[0:T, b, :], y[:, b, :], mv[0:T, b, 0:1], rstd[0:T, b:b + 1],
                                        ALU.subtract, ALU.mult).then_inc(normed, 1)

        @block.gpsimd
        def _(pool):
            pool.wait_ge(aggr, B)
            nc.gpsimd.tensor_scalar(rstd[0:T, :], mv[0:T, :, 1], EPS, None, ALU.add).then_inc(rooted, 1)
            pool.wait_ge(rooted, 1)
            nc.gpsimd.tensor_tensor(rstd[0:T, :], rstd[0:T, :], minus_half[0:T, :].to_broadcast([T, B]),
                                    ALU.pow).then_inc(rooted, 1)

        @block.sync
        def _(sp):
            for b in range(B):
                sp.wait_ge(normed, b + 1)
                sp.dma_start(out[b], x[0:T, b, :]).then_inc(stored, 16)
            sp.wait_ge(stored, 16 * B)


def kernel(**inputs):
    import concourse.bacc as _bacc
    from concourse.bass_utils import run_bass_kernel_spmd as _run

    nc = _bacc.Bacc("TRN2", target_bir_lowering=False, num_devices=1)
    arrays, args = {}, {}
    for name, value in list(inputs.items()) + list(constants().items()):
        a = np.ascontiguousarray(value)
        arrays[f"in_{name}_dram"] = a
        args[name] = nc.dram_tensor(f"in_{name}_dram", a.shape, mybir.dt.from_np(a.dtype), kind="ExternalInput").ap()
    o = nc.dram_tensor("out_0_dram", (B, T, D), F32, kind="ExternalOutput").ap()
    program(nc, args, o)
    r = _run(nc, [arrays], core_ids=[0])
    return r.results[0]["out_0_dram"]
```

```python
from contextlib import ExitStack

import numpy as np

import concourse.bass as bass
from concourse import mybir

ALU = mybir.AluOpType
ACT = mybir.ActivationFunctionType
AX = mybir.AxisListType
F32 = mybir.dt.float32
FR = mybir.dt.float32r
BF16 = mybir.dt.bfloat16
I32 = mybir.dt.int32
U32 = mybir.dt.uint32

P = 128
B, T, D = 8, 100, 512
S = 722
NH, HD = 16, 32
C = D // P
HPC = P // HD
N = B * T
HALF = N // 2
KT = -(-S // P)
LAST = S - (KT - 1) * P
HID = 1024
HC = HID // P
E = 8
LAT = 128
EPS = 1e-5
CLAMP = 10000.0
VW = HD + 2

ROWS = {"L0_attn_bq": 0, "L0_attn_bk": 1, "L0_attn_bv": 2, "L1_xattn_bq": 3, "L1_xattn_bk": 5,
        "L1_xattn_bv": 7, "L0_ffn_b1": 9, "L0_ffn_b2": 17, "L0_ffn_b3": 25}
NROWS = 33


def constants():
    f = np.float32
    theta = (f(5000.0) ** (f(-2.0) * np.arange(HD // 2, dtype=f) / f(HD))).astype(f)
    theta = np.tile(np.concatenate([theta, theta]), HPC)
    angle = (np.arange(1, T + 1, dtype=f)[None, :] * theta[:, None]).astype(f)
    rot = np.zeros((P, P), f)
    for h in range(HPC):
        for d in range(HD // 2):
            rot[h * HD + d + HD // 2, h * HD + d] = -1.0
            rot[h * HD + d, h * HD + d + HD // 2] = 1.0
    q = np.arange(T)
    causal = np.where(q[None, :] <= q[:, None], 0.0, -1e30).astype(f)
    decay = np.exp(f(-0.01 * 0.01) * np.abs(q[:, None] - q[None, :]).astype(f)).astype(f)
    return {"ident": np.eye(P, dtype=f), "cos": np.cos(angle), "sin": np.sin(angle), "rot": rot,
            "causal": causal, "decay": decay,
            "iota8": np.tile(np.arange(E, dtype=f), (P, 1))}


def three(aH, aL, bH, bL):
    return [(aH, bH), (aH, bL), (aL, bH)]


class Pair:

    def __init__(self, hi, lo):
        self.hi, self.lo = hi, lo

    def __getitem__(self, key):
        return Pair(self.hi[key], self.lo[key])


def times(a, b):
    return three(a.hi, a.lo, b.hi, b.lo)


def emit_products(pe, out, products):
    for n, (a, b) in enumerate(products):
        last = pe.matmul(out, a, b, start=(n == 0), stop=(n == len(products) - 1))
    return last


def program(nc, g, out):
    ctx = ExitStack()
    with ctx:
        def sb(name, shape, dt=F32, where=ctx):
            return where.enter_context(nc.sbuf_tensor(name, shape, dt))

        def pair(name, shape, where=ctx):
            return Pair(sb(name + "_hi", shape, FR, where), sb(name + "_lo", shape, FR, where))

        held = []

        def sem(name):
            held.append(nc.alloc_semaphore(name=name))
            return held[-1]

        def free_semaphores():
            nc.clear_and_free_semaphores(held)
            nc.all_engine_barrier()
            held.clear()

        ps = ctx.enter_context(nc.psum_tensor("ps", [P, 8, 512], F32))
        ident = sb("ident", [P, P])
        identR = sb("identR", [P, P], FR)
        BT = sb("bias_turned", [P, C, NROWS])
        x = sb("x", [P, B, D])
        xT = pair("xT", [P, C, N])
        stats = sb("stats", [P, B, 6])
        mv = sb("mean_var", [P, B, 2])
        rstd = sb("rstd", [P, B])
        bo_rows = sb("bo_rows", [P, D])

        def product_stage(name, jobs, banks=8, first=0):
            filled, hi_done, lo_done = sem(name + "_filled"), sem(name + "_hi"), sem(name + "_lo")
            with nc.Block() as block:
                @block.tensor
                def _(pe):
                    for n, (emit, view, *_r) in enumerate(jobs):
                        if n >= banks:
                            pe.wait_ge(lo_done, n - banks + 1)
                        emit(nc.tensor, view(ps[:, first + n % banks, :])).then_inc(filled, 1)

                @block.scalar
                def _(act):
                    for n, (emit, view, dst, bias, scale) in enumerate(jobs):
                        act.wait_ge(filled, n + 1)
                        src = view(ps[:, first + n % banks, :])
                        to = dst.hi if isinstance(dst, Pair) else dst
                        nc.scalar.activation(to, src, ACT.Identity, bias=0.0 if bias is None else bias,
                                             scale=scale).then_inc(hi_done, 1)

                @block.vector
                def _(dve):
                    for n, (emit, view, dst, bias, scale) in enumerate(jobs):
                        dve.wait_ge(hi_done, n + 1)
                        if not isinstance(dst, Pair):
                            if n:
                                dve.wait_ge(lo_done, n)
                            dve.sem_inc(lo_done, 1)
                            continue
                        src = view(ps[:, first + n % banks, :])
                        if scale != 1.0:
                            assert bias is None
                            nc.vector.scalar_tensor_tensor(dst.lo, src, scale, dst.hi.bitcast(F32),
                                                           ALU.mult, ALU.subtract).then_inc(lo_done, 1)
                        elif bias is not None:
                            nc.vector.scalar_tensor_tensor(dst.lo, src, bias, dst.hi.bitcast(F32),
                                                           ALU.add, ALU.subtract).then_inc(lo_done, 1)
                        else:
                            nc.vector.tensor_tensor(dst.lo, src, dst.hi.bitcast(F32),
                                                    ALU.subtract).then_inc(lo_done, 1)

        def tile_job(products, dst, rows=P, cols=HALF, bias=None, scale=1.0):
            return (lambda pe, bank: emit_products(pe, bank, products),
                    lambda bank: bank[0:rows, 0:cols], dst, bias, scale)

        def flip_job(blocks, dst, rows=P, cols=512, bias=None):
            def emit(pe, bank):
                for col, src in blocks:
                    k, m = src.shape[0], src.shape[-1]
                    last = pe.transpose(bank[0:m, col:col + k], src, ident[0:k, 0:k])
                return last
            return (emit, lambda bank: bank[0:rows, 0:cols], dst, bias, 1.0)

        def turn_weight(w, dst, nrow=C, ncol=C):
            res = []
            for c in range(ncol):
                for r0 in range(0, nrow, 4):
                    rn = min(4, nrow - r0)
                    res.append(flip_job([(k * P, w[:, r0 + k, c * P:(c + 1) * P]) for k in range(rn)],
                                        dst[:, c, r0 * P:(r0 + rn) * P], cols=rn * P))
            return res

        def project(wT, src, dst, bias=None, scale=1.0, kc=C, mc=C):
            res = []
            for m in range(mc):
                for h in range(2):
                    products = []
                    for k in range(kc):
                        products += times(wT[:, k, m * P:(m + 1) * P],
                                          src[:, k, h * HALF:(h + 1) * HALF])
                    res.append(tile_job(products, dst[:, m, h * HALF:(h + 1) * HALF],
                                        bias=None if bias is None else bias(m), scale=scale))
            return res

        def split_stage(name, items):
            hi_done, lo_done = sem(name + "_hi"), sem(name + "_lo")
            with nc.Block() as block:
                @block.scalar
                def _(act):
                    for to, src in items:
                        nc.scalar.activation(to.hi, src, ACT.Identity).then_inc(hi_done, 1)

                @block.vector
                def _(dve):
                    for n, (to, src) in enumerate(items):
                        dve.wait_ge(hi_done, n + 1)
                        nc.vector.tensor_tensor(to.lo, src, to.hi.bitcast(F32),
                                                ALU.subtract).then_inc(lo_done, 1)

        def fold_stage(name, chunks, a_rows, b_rows, dst, b_pair=None, extras=(), extra_jobs=()):
            where = ExitStack()
            RAW = 3
            ra = sb(name + "_ra", [P, RAW, D], F32, where)
            rb = sb(name + "_rb", [P, RAW, D], F32, where)
            pa, pb = pair(name + "_pa", [P, RAW, D], where), pair(name + "_pb", [P, RAW, D], where)
            landed = [sem(f"{name}_landed{i}") for i in range(RAW)]
            hi_done, lo_done, through, out_hi, out_lo, extra_s = (sem(f"{name}_{s}") for s in (
                "hi", "lo", "through", "out_hi", "out_lo", "extra"))
            both = 1 if b_pair is not None else 2
            with nc.Block() as block:
                @block.sync
                def _(sp):
                    for k in range(chunks):
                        if k >= RAW:
                            sp.wait_ge(through, k - RAW + 1)
                        sp.dma_start(ra[:, k % RAW, :], a_rows(k)).then_inc(landed[k % RAW], 16)
                        if b_pair is None:
                            sp.dma_start(rb[:, k % RAW, :], b_rows(k)).then_inc(landed[k % RAW], 16)

                @block.scalar
                def _(act):
                    for k in range(chunks):
                        s = k % RAW
                        act.wait_ge(landed[s], 16 * both * (k // RAW + 1))
                        if k >= RAW:
                            act.wait_ge(through, k - RAW + 1)
                        nc.scalar.activation(pa.hi[:, s, :], ra[:, s, :], ACT.Identity).then_inc(hi_done, 1)
                        if b_pair is None:
                            nc.scalar.activation(pb.hi[:, s, :], rb[:, s, :], ACT.Identity).then_inc(hi_done, 1)
                    act.wait_ge(through, chunks)
                    for m in range(C):
                        nc.scalar.activation(dst.hi[:, m, :], ps[:, m, :], ACT.Identity).then_inc(out_hi, 1)
                    for to, src in extra_jobs:
                        nc.scalar.activation(to.hi if isinstance(to, Pair) else to, src,
                                             ACT.Identity).then_inc(extra_s, 1)

                @block.vector
                def _(dve):
                    for k in range(chunks):
                        s = k % RAW
                        dve.wait_ge(hi_done, both * k + 1)
                        nc.vector.tensor_tensor(pa.lo[:, s, :], ra[:, s, :], pa.hi[:, s, :].bitcast(F32),
                                                ALU.subtract).then_inc(lo_done, 1)
                        if b_pair is None:
                            dve.wait_ge(hi_done, both * k + 2)
                            nc.vector.tensor_tensor(pb.lo[:, s, :], rb[:, s, :], pb.hi[:, s, :].bitcast(F32),
                                                    ALU.subtract).then_inc(lo_done, 1)
                    for m in range(C):
                        dve.wait_ge(out_hi, m + 1)
                        nc.vector.tensor_tensor(dst.lo[:, m, :], ps[:, m, :], dst.hi[:, m, :].bitcast(F32),
                                                ALU.subtract).then_inc(out_lo, 1)
                    if extra_jobs:
                        dve.wait_ge(extra_s, len(extra_jobs))
                    for n, (to, src) in enumerate(extra_jobs):
                        if isinstance(to, Pair):
                            nc.vector.tensor_tensor(to.lo, src, to.hi.bitcast(F32), ALU.subtract).then_inc(out_lo, 1)

                @block.tensor
                def _(pe):
                    for k in range(chunks):
                        s = k % RAW
                        pe.wait_ge(lo_done, both * (k + 1))
                        b_ = b_pair[:, k, :] if b_pair is not None else pb[:, s, :]
                        for m in range(C):
                            products = times(pa[:, s, m * P:(m + 1) * P], b_)
                            for n, (l, r) in enumerate(products):
                                mm = nc.tensor.matmul(ps[:, m, :], l, r, start=(k == 0 and n == 0),
                                                      stop=(k == chunks - 1 and n == 2))
                        for n, (column, rows_, lhs, rhs) in enumerate(extras):
                            mm = nc.tensor.matmul(ps[0:rows_, C, column:column + 1], lhs(k, ra[:, s, :], rb[:, s, :]),
                                                  rhs(k), start=(k == 0 and n == 0), stop=(k == chunks - 1),
                                                  skip_group_check=True)
                        mm.then_inc(through, 1)
            where.close()

        def issue_stage(name, groups):
            landed = [nc.alloc_semaphore(name=f"{name}{i}") for i in range(len(groups))]
            with nc.Block() as block:
                @block.sync
                def _(sp):
                    for s, loads in zip(landed, groups):
                        for dst, src in loads:
                            sp.dma_start(dst, src).then_inc(s, 16)
            return [(s, 16 * len(loads)) for s, loads in zip(landed, groups)]

        def await_stage(landed):
            with nc.Block() as block:
                @block.sync
                def _(sp):
                    sp.wait_ge(*landed)

        def norm_stage(name, emit, residual, gain=None, turned=True, z=None):
            made, added, stat, aggr = (sem(f"{name}_{s}") for s in ("made", "added", "stat", "aggr"))
            rooted, normed, turned_s, hi_done, lo_done = (
                sem(f"{name}_{s}") for s in ("rooted", "normed", "turned", "hi", "lo"))
            with nc.Block() as block:
                @block.tensor
                def _(pe):
                    def flips(b):
                        pe.wait_ge(normed, b + 1)
                        if b >= 2:
                            pe.wait_ge(lo_done, b - 1)
                        for c in range(C):
                            mm = nc.tensor.transpose(ps[:, 4 + b % 2, c * T:(c + 1) * T],
                                                     x[0:T, b, c * P:(c + 1) * P], ident[0:T, 0:T])
                        mm.then_inc(turned_s, 1)

                    for b in range(B):
                        if b >= 4:
                            pe.wait_ge(added, b - 3)
                        emit(nc.tensor, ps[0:T, b % 4, :], b).then_inc(made, 1)
                        if turned and b >= 2:
                            flips(b - 2)
                    if turned:
                        flips(B - 2)
                        flips(B - 1)

                @block.vector
                def _(dve):
                    def first(b):
                        dve.wait_ge(made, b + 1)
                        if gain is None:
                            nc.vector.tensor_tensor(x[0:T, b, :], ps[0:T, b % 4, :], residual[0:T, b, :],
                                                    ALU.add).then_inc(added, 1)
                        else:
                            col, rows = gain(b)
                            nc.vector.scalar_tensor_tensor(z[0:T, b % 2, :], rows, col, ps[0:T, b % 4, :],
                                                           ALU.mult, ALU.add).then_inc(aggr, 1)
                            dve.wait_ge(aggr, 2 * b + 1)
                            nc.vector.tensor_tensor(x[0:T, b, :], z[0:T, b % 2, :], residual[0:T, b, :],
                                                    ALU.add).then_inc(added, 1)
                        dve.wait_ge(added, b + 1)
                        nc.vector.bn_stats(stats[0:T, b, :], x[0:T, b, :]).then_inc(stat, 1)
                        dve.wait_ge(stat, b + 1)
                        nc.vector.bn_aggr(mv[0:T, b, :], stats[0:T, b, :]).then_inc(aggr, 1)

                    def second(b):
                        dve.wait_ge(rooted, 2 * b + 2)
                        nc.vector.tensor_scalar(x[0:T, b, :], x[0:T, b, :], mv[0:T, b, 0:1], rstd[0:T, b:b + 1],
                                                ALU.subtract, ALU.mult).then_inc(normed, 1)

                    def third(b):
                        dve.wait_ge(hi_done, b + 1)
                        nc.vector.tensor_tensor(xT.lo[:, :, b * T:(b + 1) * T],
                                                ps[:, 4 + b % 2, 0:C * T].rearrange("p (c t) -> p c t", c=C),
                                                xT.hi[:, :, b * T:(b + 1) * T].bitcast(F32),
                                                ALU.subtract).then_inc(lo_done, 1)

                    for b in range(B + 3):
                        if b < B:
                            first(b)
                        if 1 <= b <= B:
                            second(b - 1)
                        if turned and b >= 3:
                            third(b - 3)

                @block.gpsimd
                def _(pool):
                    per = 2 if gain is not None else 1
                    for b in range(B):
                        pool.wait_ge(aggr, per * (b + 1))
                        nc.gpsimd.tensor_scalar(rstd[0:T, b:b + 1], mv[0:T, b, 1:2], EPS, None,
                                                ALU.add).then_inc(rooted, 1)
                        pool.wait_ge(rooted, 2 * b + 1)
                        nc.gpsimd.tensor_tensor(rstd[0:T, b:b + 1], rstd[0:T, b:b + 1], minus_half[0:T, :],
                                                ALU.pow).then_inc(rooted, 1)

                @block.scalar
                def _(act):
                    if turned:
                        for b in range(B):
                            act.wait_ge(turned_s, b + 1)
                            nc.scalar.activation(xT.hi[:, :, b * T:(b + 1) * T],
                                                 ps[:, 4 + b % 2, 0:C * T].rearrange("p (c t) -> p c t", c=C),
                                                 ACT.Identity).then_inc(hi_done, 1)

        minus_half = sb("minus_half", [P, 1])
        hid = lambda a: a.rearrange("(c p) d -> p c d", p=P)
        natural = lambda w, r=C: w.rearrange("(r p) i -> p r i", p=P)

        gw = sb("gate_w", [P, C, E])
        gb = sb("gate_b", [E, 1])
        iota8 = sb("iota8", [P, E])
        ph = ExitStack()
        cos, sin, rot = sb("cos", [P, T], F32, ph), sb("sin", [P, T], F32, ph), sb("rot", [P, P], F32, ph)
        causal = sb("causal", [T, C, T], FR, ph)
        wo = pair("l0_wo", [P, C, D], ph)
        qp, kf = pair("q_roped", [P, C, N], ph), sb("k_roped", [P, C, N], F32, ph)
        v = pair("l0_v", [T, B, NH, VW], ph)
        wst = ExitStack()
        wq, wk, wv = (pair("l0_" + n, [P, C, D], wst) for n in ("wq", "wk", "wv"))
        rst = ExitStack()
        raw = [sb(f"l0_raw{i}", [P, C, D], F32, rst) for i in range(3)]
        raw.append(kf[:, :, 0:D])
        causal_f = kf[0:T, 0, D:D + T]
        rows = bo_rows[0:NROWS, :]
        loads = []
        for key, at in ROWS.items():
            table = g[key]
            n = table.shape[0] if len(table.shape) == 2 else table.shape[0] // D
            if len(table.shape) == 1:
                table = table.rearrange("(r i) -> r i", i=D)
            loads.append((rows[at:at + n, :], table))
        started = sem("started")
        in_x, in_w, in_rest = issue_stage("in_start", [
            [(ident[:], g["ident"])] + loads + [(x[0:T, b, :], g["x"][b]) for b in range(B)],
            [(raw[i][:], natural(g["L0_attn_" + key])) for i, key in enumerate(("Wq", "Wk", "Wv"))],
            [(causal_f, g["causal"]), (cos[:], g["cos"]), (sin[:], g["sin"]), (rot[:], g["rot"]),
             (raw[3], natural(g["L0_attn_Wo"])), (gw[:], g["L0_ffn_gate_w"].rearrange("(c p) e -> p c e", p=P)),
             (gb[:], g["L0_ffn_gate_b"].unsqueeze(1)), (iota8[:], g["iota8"])]])
        with nc.Block() as block:
            @block.vector
            def _(dve):
                nc.vector.memset(minus_half[:], -0.5).then_inc(started, 1)
                nc.vector.memset(v.hi[:, :, :, HD:HD + 1].bitcast(F32), 1.0).then_inc(started, 1)
                nc.vector.memset(v.hi[:, :, :, HD + 1:].bitcast(F32), 0.0).then_inc(started, 1)
                nc.vector.memset(v.lo[:, :, :, HD:].bitcast(F32), 0.0).then_inc(started, 1)
                dve.wait_ge(*in_x)
                nc.vector.tensor_copy(identR[:], ident[:]).then_inc(started, 1)

        jobs = [flip_job([(c * NROWS, rows[:, c * P:(c + 1) * P]) for c in range(C)],
                         BT[:, :, :].rearrange("p c r -> p (c r)"), cols=C * NROWS)]
        for b in range(B):
            def emit(pe, view, b=b):
                for c in range(C):
                    last = pe.transpose(view[:, c, :], x[0:T, b, c * P:(c + 1) * P], ident[0:T, 0:T])
                return last
            jobs.append((emit, lambda bank: bank[:, 0:C * T].rearrange("p (c t) -> p c t", c=C),
                         xT[:, :, b * T:(b + 1) * T], None, 1.0))
        product_stage("turn_x", jobs)

        def add_bias(rows_landed, done):
            nc.gpsimd.wait_ge(rows_landed, 16)
            for b in range(B):
                nc.gpsimd.tensor_tensor(x[0:T, b, :], x[0:T, b, :], bo_rows[0:T, :], ALU.add).then_inc(done, 1)

        def attention_stage(name, q, k, v, yT, scale, masked, decay, phase, rows_landed=None):
            kd = pair(name + "_kd", [P, 2, C, HPC, T], phase)
            E_ = sb(name + "_e", [T, 2, NH, T], F32, phase)
            mx = sb(name + "_mx", [T, 2, NH], F32, phase)
            aT = pair(name + "_aT", [T, 2, NH, T], phase)
            rec = sb(name + "_rec", [T, 2, NH], F32, phase)
            y = sb(name + "_y", [T, 2, NH, HD], F32, phase)
            (zeroed, kd_hi, kd_lo, sc, clip, faded, red, sub, ex, tp, thi, tlo, pv, rc, yn) = (
                sem(f"{name}_{s}") for s in (
                    "zeroed", "kd_hi", "kd_lo", "scores", "clip", "decayed", "max", "less", "exp", "turned",
                    "t_hi", "t_lo", "values", "reciprocal", "y"))
            residual = sem(name + "_residual")
            order = []
            for b in range(B):
                order += [("w", b, c) for c in range(C)] + ([("y", b - 1, 0)] if b else [])
            order.append(("y", B - 1, 0))
            at = {key: n for n, key in enumerate(order)}
            bank = lambda key: ps[:, 4 + at[key] % 2, 0:C * T]
            with nc.Block() as block:
                @block.tensor
                def _(pe):
                    def scores(b):
                        for c in range(C):
                            if c == 0:
                                pe.wait_ge(kd_lo, HPC * (b + 1))
                            if b >= 1 and c % 2 == 0:
                                pe.wait_ge(sub, 2 * (b - 1) + c // 2 + 1)
                            if masked:
                                nc.tensor.matmul(ps[0:T, c, 0:HPC * T], identR[0:T, 0:T],
                                                 causal[:, :, :].rearrange("q c k -> q (c k)"),
                                                 start=True, stop=False, skip_group_check=True)
                            products = times(q[:, c, b * T:(b + 1) * T],
                                             Pair(*(t[:, b % 2, c, :, :].rearrange("p r t -> p (r t)")
                                                    for t in (kd.hi, kd.lo))))
                            for n, (l, r) in enumerate(products):
                                mm = nc.tensor.matmul(ps[0:T, c, 0:HPC * T], l, r, start=(n == 0 and not masked),
                                                      stop=(n == 2), skip_group_check=True)
                            if c % 2:
                                mm.then_inc(sc, 1)

                    def turn(b):
                        for c in range(C):
                            n = at["w", b, c]
                            pe.wait_ge(ex, 2 * b + c // 2 + 1)
                            if n >= 2:
                                pe.wait_ge(tlo, n - 1)
                            for r in range(HPC):
                                mm = nc.tensor.transpose(bank(("w", b, c))[0:T, r * T:(r + 1) * T],
                                                         E_[:, b % 2, c * HPC + r, :], ident[0:T, 0:T])
                            mm.then_inc(tp, 1)

                    def values(b):
                        pe.wait_ge(tlo, at["w", b, C - 1] + 1)
                        if b >= 1:
                            pe.wait_ge(yn, b)
                        for h in range(NH):
                            mm = emit_products(nc.tensor, ps[0:T, 6 + h // 8, h % 8 * VW:(h % 8 + 1) * VW],
                                               times(aT[:, b % 2, h, :], v[:, b, h, :]))
                        mm.then_inc(pv, 1)

                    def turn_y(b):
                        n = at["y", b, 0]
                        pe.wait_ge(yn, b + 1)
                        pe.wait_ge(tlo, n - 1)
                        for c in range(C):
                            mm = nc.tensor.transpose(
                                bank(("y", b, 0))[:, c * T:(c + 1) * T],
                                y[:, b % 2, c * HPC:(c + 1) * HPC, :].rearrange("t h d -> t (h d)"),
                                ident[0:T, 0:T])
                        mm.then_inc(tp, 1)

                    scores(0)
                    for b in range(B):
                        turn(b)
                        if b + 1 < B:
                            scores(b + 1)
                        if b >= 1:
                            turn_y(b - 1)
                        values(b)
                    turn_y(B - 1)

                def source(key):
                    rows_ = T if key[0] == "w" else P
                    return bank(key)[0:rows_, :].rearrange("p (c t) -> p c t", c=C)

                def target(key):
                    kind, b, c = key
                    return aT[:, b % 2, c * HPC:(c + 1) * HPC, :] if kind == "w" else yT[:, :, b * T:(b + 1) * T]

                @block.vector
                def _(dve):
                    def soft(b, h):
                        s = ps[0:T, 2 * h:2 * h + 2, 0:HPC * T].rearrange("q c (r k) -> q c r k", r=HPC)
                        heads = slice(8 * h, 8 * h + 8)
                        e = E_[:, b % 2, heads, :]
                        m = mx[:, b % 2, heads]
                        by_bank = lambda t: t.rearrange("q (c r) k -> q c r k", c=2)
                        dve.wait_ge(sc, 2 * b + h + 1)
                        if b >= 2:
                            dve.wait_ge(tp, at["w", b - 2, 2 * h + 1] + 1)
                        if decay is not None:
                            nc.vector.tensor_scalar(e.rearrange("q (c r) k -> q c (r k)", c=2),
                                                    ps[0:T, 2 * h:2 * h + 2, 0:HPC * T],
                                                    -CLAMP, CLAMP, ALU.max, ALU.min).then_inc(clip, 1)
                            dve.wait_ge(clip, 2 * b + h + 1)
                            nc.vector.tensor_tensor(e, e, decay[:, :].unsqueeze(1).to_broadcast([T, 8, T]),
                                                    ALU.mult).then_inc(faded, 1)
                            dve.wait_ge(faded, 2 * b + h + 1)
                            nc.vector.tensor_reduce(m, e, AX.X, ALU.max).then_inc(red, 1)
                            dve.wait_ge(red, 2 * b + h + 1)
                            nc.vector.tensor_tensor(e, e, m.unsqueeze(2).to_broadcast([T, 8, T]),
                                                    ALU.subtract).then_inc(sub, 1)
                        else:
                            nc.vector.tensor_reduce(m.rearrange("q (c r) -> q c r", c=2), s, AX.X,
                                                    ALU.max).then_inc(red, 1)
                            dve.wait_ge(red, 2 * b + h + 1)
                            nc.vector.tensor_tensor(
                                by_bank(e), s, m.rearrange("q (c r) -> q c r", c=2).unsqueeze(3)
                                .to_broadcast([T, 2, HPC, T]), ALU.subtract).then_inc(sub, 1)

                    def lows(key):
                        dve.wait_ge(thi, at[key] + 1)
                        to, src = target(key), source(key)
                        if key[0] == "w" or bias_of is None:
                            nc.vector.tensor_tensor(to.lo, src, to.hi.bitcast(F32), ALU.subtract).then_inc(tlo, 1)
                        else:
                            for c in range(C):
                                ins = nc.vector.scalar_tensor_tensor(
                                    to.lo[:, c, :], src[:, c, :], bias_of(c), to.hi[:, c, :].bitcast(F32),
                                    ALU.add, ALU.subtract)
                            ins.then_inc(tlo, 1)

                    def outputs(b):
                        o = ps[0:T, 6:8, 0:8 * VW].rearrange("q i (h d) -> q i h d", h=8)
                        half = lambda t: t.rearrange("q (i h) -> q i h", i=2)
                        dve.wait_ge(pv, b + 1)
                        nc.vector.reciprocal(half(rec[:, b % 2, :]).unsqueeze(3), o[:, :, :, HD:HD + 1]).then_inc(rc, 1)
                        dve.wait_ge(rc, b + 1)
                        if b >= 2:
                            dve.wait_ge(tp, at["y", b - 2, 0] + 1)
                        nc.vector.tensor_tensor(
                            y[:, b % 2, :, :].rearrange("q (i h) d -> q i h d", i=2), o[:, :, :, 0:HD],
                            half(rec[:, b % 2, :]).unsqueeze(3).to_broadcast([T, 2, 8, HD]), ALU.mult).then_inc(yn, 1)

                    for i in range(2):
                        for t in (kd.hi, kd.lo):
                            nc.vector.memset(t[:, i].bitcast(F32), 0.0).then_inc(zeroed, 1)
                    soft(0, 0)
                    soft(0, 1)
                    for b in range(B):
                        for c in range(C):
                            if b >= 1 and c == 2:
                                outputs(b - 1)
                            lows(("w", b, c))
                        if b + 1 < B:
                            soft(b + 1, 0)
                        if b >= 1:
                            lows(("y", b - 1, 0))
                        if b + 1 < B:
                            soft(b + 1, 1)
                    outputs(B - 1)
                    lows(("y", B - 1, 0))

                def diagonal(t, b, r):
                    return t[r * HD:(r + 1) * HD, b % 2, :, r, :]

                def head_keys(b, r):
                    return k[r * HD:(r + 1) * HD, :, b * T:(b + 1) * T]

                @block.scalar
                def _(act):
                    def keys_hi(b):
                        for r in range(HPC):
                            if b < 2 and r == 0:
                                act.wait_ge(zeroed, 2 * b + 2)
                            if b >= 2 and r == 0:
                                act.wait_ge(sc, 2 * (b - 1))
                            nc.scalar.activation(diagonal(kd.hi, b, r), head_keys(b, r), ACT.Identity
                                                 ).then_inc(kd_hi, 1)

                    def expo(b, h):
                        act.wait_ge(sub, 2 * b + h + 1)
                        e = E_[:, b % 2, 8 * h:8 * h + 8, :]
                        nc.scalar.activation(e, e, ACT.Exp, scale=scale).then_inc(ex, 1)

                    def highs(key):
                        kind, b, c = key
                        act.wait_ge(tp, at[key] + 1)
                        if kind == "w" and b >= 2 and c == 0:
                            act.wait_ge(pv, b - 1)
                        to, src = target(key).hi, source(key)
                        if kind == "w" or bias_of is None:
                            nc.scalar.activation(to, src, ACT.Identity).then_inc(thi, 1)
                        else:
                            for c in range(C):
                                ins = nc.scalar.activation(to[:, c, :], src[:, c, :], ACT.Identity, bias=bias_of(c))
                            ins.then_inc(thi, 1)

                    keys_hi(0)
                    keys_hi(1)
                    expo(0, 0)
                    expo(0, 1)
                    for b in range(B):
                        for c in range(C):
                            highs(("w", b, c))
                        if b + 2 < B:
                            keys_hi(b + 2)
                        if b >= 1:
                            highs(("y", b - 1, 0))
                        if b + 1 < B:
                            expo(b + 1, 0)
                            expo(b + 1, 1)
                    highs(("y", B - 1, 0))

                @block.gpsimd
                def _(pool):
                    for b in range(B):
                        for r in range(HPC):
                            pool.wait_ge(kd_hi, HPC * b + r + 1)
                            nc.gpsimd.tensor_tensor(diagonal(kd.lo, b, r), head_keys(b, r),
                                                    diagonal(kd.hi, b, r).bitcast(F32), ALU.subtract).then_inc(kd_lo, 1)
                    if rows_landed is not None:
                        pool.wait_ge(kd_lo, HPC * B)
                        add_bias(rows_landed, residual)

        await_stage(in_w)
        product_stage("turn_w0", turn_weight(raw[0], wq) + turn_weight(raw[1], wk) + turn_weight(raw[2], wv))
        bo0_landed, = issue_stage("in_bo0", [[(bo_rows[:], g["L0_attn_bo"].partition_broadcast(P))]])
        masked = sem("mask")
        with nc.Block() as block:
            @block.vector
            def _(dve):
                dve.wait_ge(*in_rest)
                nc.vector.tensor_copy(causal[:], causal_f.unsqueeze(1).to_broadcast([T, C, T])).then_inc(masked, 1)

        def value_jobs(srcT, w, dst, kc=C):
            res = []
            for b in range(B):
                products = []
                for k in range(kc):
                    products += times(srcT[:, k, b * T:(b + 1) * T], w[:, k, :])

                def emit(pe, bank, products=products):
                    return emit_products(pe, bank.rearrange("q h d -> q (h d)"), products)
                res.append((emit, lambda bank: bank[0:T, :].rearrange("q (h d) -> q h d", h=NH),
                            dst[:, b, :, 0:HD], None, 1.0))
            return res

        brow = lambda key, extra=0: (lambda m: BT[:, m, ROWS[key] + extra:ROWS[key] + extra + 1])
        product_stage("qkv0", turn_weight(raw[3], wo) + value_jobs(xT, wv, v))
        rst.close()

        def rope_stage():
            made, biased, swapped, t1s, t2s, added, q_hi, q_lo = (sem("rope_" + s) for s in (
                "made", "biased", "swapped", "t1", "t2", "added", "q_hi", "q_lo"))
            t1, t2 = sb("rope_t1", [P, 2, HALF], F32, wst), sb("rope_t2", [P, 2, HALF], F32, wst)
            f = sb("rope_f", [P, 4, HALF], F32, wst)
            jobs = [(w, m, h, q) for w, q in ((wq, True), (wk, False)) for m in range(C) for h in range(2)]
            NQ = len(jobs) // 2
            table = lambda t: t[:, :].unsqueeze(1).to_broadcast([P, HALF // T, T])
            by_batch = lambda a: a.rearrange("p (b t) -> p b t", t=T)
            with nc.Block() as block:
                @block.tensor
                def _(pe):
                    def swap(n):
                        pe.wait_ge(biased, n + 1)
                        if n >= 4:
                            pe.wait_ge(t2s, n - 3)
                        nc.tensor.matmul(ps[:, 4 + n % 4, 0:HALF], rot[:, :], f[:, n % 4, :],
                                         start=True, stop=True).then_inc(swapped, 1)
                    for n, (w, m, h, q) in enumerate(jobs):
                        if n >= 4:
                            pe.wait_ge(biased, n - 3)
                        products = []
                        for k in range(C):
                            products += times(w[:, k, m * P:(m + 1) * P], xT[:, k, h * HALF:(h + 1) * HALF])
                        emit_products(nc.tensor, ps[:, n % 4, 0:HALF], products).then_inc(made, 1)
                        if n >= 1:
                            swap(n - 1)
                    swap(len(jobs) - 1)

                @block.scalar
                def _(act):
                    def high(n):
                        w, m, h, q = jobs[n]
                        act.wait_ge(added, n + 1)
                        nc.scalar.activation(qp.hi[:, m, h * HALF:(h + 1) * HALF], f[:, n % 4, :],
                                             ACT.Identity).then_inc(q_hi, 1)

                    for n, (w, m, h, q) in enumerate(jobs):
                        act.wait_ge(made, n + 1)
                        if n >= 4:
                            act.wait_ge(added, n - 3)
                            act.wait_ge(q_lo, min(n - 3, NQ))
                        nc.scalar.activation(f[:, n % 4, :], ps[:, n % 4, 0:HALF], ACT.Identity,
                                             bias=brow("L0_attn_bq" if q else "L0_attn_bk")(m)).then_inc(biased, 1)
                        if 2 <= n < NQ + 2:
                            high(n - 2)

                @block.gpsimd
                def _(pool):
                    for n in range(len(jobs)):
                        pool.wait_ge(biased, n + 1)
                        if n >= 2:
                            pool.wait_ge(added, n - 1)
                        nc.gpsimd.tensor_tensor(by_batch(t1[:, n % 2, :]), by_batch(f[:, n % 4, :]),
                                                table(cos), ALU.mult).then_inc(t1s, 1)

                @block.vector
                def _(dve):
                    def low(n):
                        w, m, h, q = jobs[n]
                        dve.wait_ge(q_hi, n + 1)
                        to = qp[:, m, h * HALF:(h + 1) * HALF]
                        nc.vector.tensor_tensor(to.lo, f[:, n % 4, :], to.hi.bitcast(F32),
                                                ALU.subtract).then_inc(q_lo, 1)

                    for n, (w, m, h, q) in enumerate(jobs):
                        dve.wait_ge(swapped, n + 1)
                        if n >= 2:
                            dve.wait_ge(added, n - 1)
                        nc.vector.tensor_tensor(by_batch(t2[:, n % 2, :]), by_batch(ps[:, 4 + n % 4, 0:HALF]),
                                                table(sin), ALU.mult).then_inc(t2s, 1)
                        dve.wait_ge(t2s, n + 1)
                        dve.wait_ge(t1s, n + 1)
                        to = f[:, n % 4, :] if q else kf[:, m, h * HALF:(h + 1) * HALF]
                        nc.vector.tensor_tensor(to, t1[:, n % 2, :], t2[:, n % 2, :], ALU.add).then_inc(added, 1)
                        if 1 <= n < NQ + 1:
                            low(n - 1)
        rope_stage()
        wst.close()
        yT = xT
        att = ExitStack()
        bias_of = brow("L0_attn_bv")
        attention_stage("att0", qp, kf, v, yT, float(HD) ** -0.5, True, None, att, bo0_landed[0])
        att.close()
        norm_stage("norm0", lambda pe, bank, b: emit_products(pe, bank, [
            p for k in range(C) for p in times(yT[:, k, b * T:(b + 1) * T], wo[:, k, :])]), x)
        ph.close()
        free_semaphores()

        def float8_steps(dst, v_, m_):
            return [
                lambda: nc.vector.tensor_scalar(m_.bitcast(I32), v_.bitcast(I32), 0x7F800000, None, ALU.bitwise_and),
                lambda: nc.vector.tensor_scalar(m_, m_, 2.0 ** -6, 1.5 * 2.0 ** 20, ALU.max, ALU.mult),
                lambda: nc.vector.tensor_tensor(v_, v_, m_, ALU.add),
                lambda: nc.vector.tensor_tensor(v_, v_, m_, ALU.subtract),
                lambda: nc.vector.tensor_scalar(m_.bitcast(I32), v_.bitcast(I32), 0x7FFFFFFF, None, ALU.bitwise_and),
                lambda: nc.vector.tensor_scalar(m_, m_, 448.0, 3e38, ALU.is_gt, ALU.mult),
                lambda: nc.vector.scalar_tensor_tensor(dst, m_, 3e38, v_, ALU.mult, ALU.add)]

        def context_stage(name, qT, aT_out, queries_share, phase, scale, rowsum=None, qbk=None,
                          rows_landed=None, beside=None):
            raw = sb(name + "_ctx", [P, 2, KT, D], F32, phase)
            cn = pair(name + "_cn", [P, 2, KT, D], phase)
            ct = pair(name + "_ct", [P, C, KT * P], phase)
            pn = sb(name + "_pn", [T, S], F32, phase)
            pk = sb(name + "_pk", [P, KT, T], F32, phase) if queries_share else None
            pT = pair(name + "_pT", [P, KT, T], phase)
            a = pair(name + "_a", [T, D], phase)
            st = sb(name + "_st", [P, 4, KT], F32, phase)
            landed = [sem(f"{name}_landed{i}") for i in range(2)]
            (split_hi, split_lo, split_lo_pool, used, filled, scored, peak, less, ex, sm, even, a_done, a_hi, a_lo,
             w_hi, w_lo, ready_s, summed) = (sem(f"{name}_{s}") for s in (
                 "split_hi", "split_lo", "split_lo_pool", "used", "filled", "scored", "peak", "less", "exp",
                 "sum", "even", "a_done", "a_hi", "a_lo", "w_hi", "w_lo", "copied", "rowsum"))
            zeroed, residual = sem(name + "_zeroed"), sem(name + "_residual")
            RING = 4 if queries_share else 5
            SB, AB = 5, 7
            read = [sem(f"{name}_read{i}") for i in range(RING)]
            whole = (KT - 1) * P
            keys = lambda j: P if j < KT - 1 else LAST
            POOL_TILES = (2, 5)
            FIRST = 2
            TURN = 4 if queries_share else 5
            PARTS = ((0, P, 0, KT - 1), (1, LAST, KT - 1, KT))

            order = [("c", 0, j, part) for j in range(KT) for part in range(2)]
            order += [("p", 0, i, 0) for i in range(2)]
            for b in range(B):
                if b + 1 < B:
                    order += [("c", b + 1, j, part) for j in range(KT) for part in range(2)]
                    order += [("p", b + 1, i, 0) for i in range(2)]
                order += [("a", b, 0, part) for part in range(2)]
            at = {key: n for n, key in enumerate(order)}
            bank = lambda key: at[key] % RING

            def is_read(eng, key):
                eng.wait_ge(read[bank(key)], at[key] // RING + 1)

            def lo_ready(eng, b, j):
                if j in POOL_TILES:
                    eng.wait_ge(split_lo_pool, len(POOL_TILES) * b + POOL_TILES.index(j) + 1)
                else:
                    mine = [i for i in range(KT) if i not in POOL_TILES]
                    eng.wait_ge(split_lo, len(mine) * b + mine.index(j) + 1)

            by_part = lambda t, part: t.lo if part else t.hi
            with nc.Block() as block:
                @block.sync
                def _(sp):
                    for b in range(B):
                        if b >= 2:
                            sp.wait_ge(split_lo, (KT - len(POOL_TILES)) * (b - 1))
                            sp.wait_ge(split_lo_pool, len(POOL_TILES) * (b - 1))
                        sp.dma_start(raw[:, b % 2, 0:KT - 1, :],
                                     g["ctx_1024"][b, 0:whole, :].rearrange("(j p) d -> p j d", p=P)
                                     ).then_inc(landed[b % 2], 16)
                        sp.dma_start(raw[0:LAST, b % 2, KT - 1, :],
                                     g["ctx_1024"][b, whole:S, :]).then_inc(landed[b % 2], 16)

                @block.tensor
                def _(pe):
                    def claim(key):
                        if at[key] >= RING:
                            pe.wait_ge(read[bank(key)], at[key] // RING)
                        return ps[:, bank(key), :]

                    def turn_tile(b, j):
                        for part in range(2):
                            pe.wait_ge(split_hi, KT * b + j + 1) if part == 0 else lo_ready(pe, b, j)
                            to = claim(("c", b, j, part))
                            for c in range(C):
                                mm = nc.tensor.transpose(
                                    to[:, c * P:c * P + keys(j)].bitcast(FR),
                                    by_part(cn, part)[0:keys(j), b % 2, j, c * P:(c + 1) * P],
                                    identR[0:keys(j), 0:keys(j)])
                            mm.then_inc(filled, 1)

                    def scores(b):
                        for j in range(KT):
                            for part in range(2):
                                is_read(pe, ("c", b, j, part))
                        if b >= 1:
                            pe.wait_ge(ready_s if queries_share else ex, b)
                        for k0, w in ((0, 512), (512, S - 512)):
                            mm = emit_products(nc.tensor, ps[0:T, SB + k0 // 512, 0:w], [
                                p for k in range(C) for p in times(qT[:, k, b * T:(b + 1) * T], ct[:, k, k0:k0 + w])])
                        mm.then_inc(scored, 1)

                    def turn_p(b):
                        pe.wait_ge(ready_s if queries_share else ex, b + 1)
                        for i, rows_, j0, j1 in PARTS:
                            to = claim(("p", b, i, 0))
                            for j in range(j0, j1):
                                mm = nc.tensor.transpose(to[0:rows_, (j - j0) * T:(j - j0 + 1) * T],
                                                         pn[:, j * P:j * P + rows_], ident[0:T, 0:T])
                            mm.then_inc(filled, 1)

                    def value(b, j):
                        if j == 0:
                            if queries_share:
                                pe.wait_ge(w_lo, b + 1)
                            else:
                                for i in range(2):
                                    is_read(pe, ("p", b, i, 0))
                            if b >= 1:
                                pe.wait_ge(a_lo, b)
                        products = times(pT[0:keys(j), j, :], cn[0:keys(j), b % 2, j, :])
                        for n, (l, r) in enumerate(products):
                            mm = nc.tensor.matmul(ps[0:T, AB, :], l, r, start=(j == 0 and n == 0),
                                                  stop=(j == KT - 1 and n == 2))
                        mm.then_inc(used, 1)
                        if j == KT - 1 and rowsum is not None:
                            mm = emit_products(nc.tensor, ps[0:T, RING, 0:2], [
                                p for i in range(KT) for p in ((pT.hi[0:keys(i), i, :], ones_col[0:keys(i), :]),
                                                               (pT.lo[0:keys(i), i, :], ones_col[0:keys(i), :]))])
                            mm.then_inc(summed, 1)

                    def turn_a(b):
                        for part in range(2):
                            pe.wait_ge(a_lo if part else a_hi, b + 1)
                            to = claim(("a", b, 0, part))
                            for c in range(C):
                                mm = nc.tensor.transpose(to[:, c * T:(c + 1) * T].bitcast(FR),
                                                         by_part(a, part)[:, c * P:(c + 1) * P], identR[0:T, 0:T])
                            mm.then_inc(filled, 1)

                    for j in range(KT):
                        turn_tile(0, j)
                    scores(0)
                    turn_p(0)
                    for b in range(B):
                        more = b + 1 < B
                        if more:
                            for j in range(KT):
                                turn_tile(b + 1, j)
                        for j in range(KT):
                            if more and j == FIRST:
                                scores(b + 1)
                            if more and j == TURN:
                                turn_p(b + 1)
                            value(b, j)
                        turn_a(b)

                def ready(eng, key):
                    eng.wait_ge(filled, at[key] + 1)
                    return ps[:, bank(key), :]

                def tile_to(t, part, j):
                    return by_part(t, part)[:, :, j * P:j * P + keys(j)]

                def turned_p(eng, b, i, rows_, j0, j1):
                    return ready(eng, ("p", b, i, 0))[0:rows_, 0:(j1 - j0) * T].rearrange("p (j t) -> p j t", t=T)

                ahead = lambda b, j0, j1: range(j0, j1) if b < B else ()

                @block.scalar
                def _(act):
                    def split(b, js):
                        for j in js:
                            act.wait_ge(landed[b % 2], 32 * (b // 2 + 1))
                            if b >= 2:
                                act.wait_ge(used, KT * (b - 2) + j + 1)
                            nc.scalar.activation(cn.hi[0:keys(j), b % 2, j, :], raw[0:keys(j), b % 2, j, :],
                                                 ACT.Identity).then_inc(split_hi, 1)

                    def turned(b, js):
                        for j in js:
                            src = ready(act, ("c", b, j, 0))[:, :].rearrange("p (c k) -> p c k", c=C)[:, :, 0:keys(j)]
                            if b >= 1 and j == 0:
                                act.wait_ge(scored, b)
                            nc.scalar.activation(tile_to(ct, 0, j), src, ACT.Identity
                                                 ).then_inc(read[bank(("c", b, j, 0))], 1)

                    def scores_out(b):
                        act.wait_ge(scored if queries_share else less, b + 1)
                        if b >= 1:
                            act.wait_ge(filled, at[("p", b - 1, 1, 0)] + 1)
                        src = ps[0:T, SB:SB + 2, :].rearrange("q i k -> q (i k)")[:, 0:S]
                        if queries_share:
                            nc.scalar.activation(pn[:, :], src, ACT.Identity, bias=qbk[:, b:b + 1]).then_inc(ready_s, 1)
                        else:
                            if b >= 1:
                                act.wait_ge(sm, b)
                            nc.scalar.activation(pn[:, :], src, ACT.Exp, bias=st[0:T, 1, 0:1], scale=scale,
                                                 accum_out=st[0:T, 2, 0:1]).then_inc(ex, 1)

                    def weights(b):
                        if queries_share:
                            act.wait_ge(even, b + 1)
                            if b >= 1:
                                act.wait_ge(used, KT * b)
                                act.wait_ge(summed, b)
                            nc.scalar.activation(pT.hi[:], pk[:], ACT.Identity).then_inc(w_hi, 1)
                            return
                        if b >= 1:
                            act.wait_ge(used, KT * b)
                        for part in PARTS:
                            src = turned_p(act, b, *part)
                            _, rows_, j0, j1 = part
                            nc.scalar.activation(pT.hi[0:rows_, j0:j1, :], src, ACT.Identity).then_inc(w_hi, 1)

                    def expo(b):
                        for i in range(2):
                            is_read(act, ("p", b, i, 0))
                        nc.scalar.activation(pk[:], pk[:], ACT.Exp, scale=scale).then_inc(ex, 1)

                    def out_split(b):
                        act.wait_ge(used, KT * (b + 1))
                        if b >= 1:
                            act.wait_ge(filled, at[("a", b - 1, 0, 1)] + 1)
                        if not queries_share:
                            act.wait_ge(sm, b + 1)
                        nc.scalar.activation(a.hi[:, :], ps[0:T, AB, :], ACT.Identity,
                                             scale=1.0 if queries_share else st[0:T, 3, 0:1]).then_inc(a_hi, 1)

                    def out_turned(b):
                        key = ("a", b, 0, 0)
                        src = ready(act, key)[:, 0:C * T].rearrange("p (c t) -> p c t", c=C)
                        nc.scalar.activation(aT_out.hi[:, :, b * T:(b + 1) * T], src,
                                             ACT.Identity).then_inc(read[bank(key)], 1)

                    split(0, range(KT))
                    split(1, range(KT))
                    turned(0, range(KT))
                    scores_out(0)
                    if queries_share:
                        expo(0)
                    for b in range(B):
                        more = b + 1 < B
                        if queries_share:
                            turned(b + 1, ahead(b + 1, 0, 2))
                            weights(b)
                            turned(b + 1, ahead(b + 1, 2, KT))
                        else:
                            weights(b)
                            turned(b + 1, ahead(b + 1, 0, KT))
                        split(b + 2, ahead(b + 2, 0, FIRST))
                        if more:
                            scores_out(b + 1)
                        split(b + 2, ahead(b + 2, FIRST, TURN))
                        if more and queries_share:
                            expo(b + 1)
                        out_split(b)
                        split(b + 2, ahead(b + 2, TURN, KT))
                        out_turned(b)

                @block.gpsimd
                def _(pool):
                    for b in range(B):
                        for n, j in enumerate(POOL_TILES):
                            rw = keys(j)
                            pool.wait_ge(split_hi, KT * b + j + 1)
                            nc.gpsimd.tensor_tensor(cn.lo[0:rw, b % 2, j, :], raw[0:rw, b % 2, j, :],
                                                    cn.hi[0:rw, b % 2, j, :].bitcast(F32),
                                                    ALU.subtract).then_inc(split_lo_pool, 1)
                    if rows_landed is not None:
                        pool.wait_ge(split_lo_pool, len(POOL_TILES) * B)
                        add_bias(rows_landed, residual)

                @block.vector
                def _(dve):
                    def split(b, js):
                        for j in js:
                            if j not in POOL_TILES:
                                rw = keys(j)
                                dve.wait_ge(split_hi, KT * b + j + 1)
                                nc.vector.tensor_tensor(cn.lo[0:rw, b % 2, j, :], raw[0:rw, b % 2, j, :],
                                                        cn.hi[0:rw, b % 2, j, :].bitcast(F32),
                                                        ALU.subtract).then_inc(split_lo, 1)

                    def turned(b, js):
                        for j in js:
                            key = ("c", b, j, 1)
                            src = ready(dve, key)[:, :].rearrange("p (c k) -> p c k", c=C)[:, :, 0:keys(j)]
                            if b >= 1 and j == 0:
                                dve.wait_ge(scored, b)
                            nc.vector.tensor_copy(tile_to(ct, 1, j), src).then_inc(read[bank(key)], 1)

                    def peaks(b):
                        if not queries_share:
                            dve.wait_ge(scored, b + 1)
                            if b >= 1:
                                dve.wait_ge(ex, b)
                            nc.vector.tensor_reduce(st[0:T, 0, 0:1],
                                                    ps[0:T, SB:SB + 2, :].rearrange("q i k -> q (i k)")[:, 0:S],
                                                    AX.X, ALU.max).then_inc(peak, 1)
                            dve.wait_ge(peak, b + 1)
                            nc.vector.tensor_scalar(st[0:T, 1, 0:1], st[0:T, 0, 0:1], -scale, None,
                                                    ALU.mult).then_inc(less, 1)
                            return
                        for part in PARTS:
                            src = turned_p(dve, b, *part)
                            i, rows_, j0, j1 = part
                            nc.vector.tensor_reduce(st[0:rows_, 0, j0:j1], src, AX.X, ALU.max).then_inc(peak, 1)
                            dve.wait_ge(peak, 2 * b + i + 1)
                            if b >= 1 and i == 0:
                                dve.wait_ge(w_lo, b)
                            nc.vector.tensor_tensor(
                                pk[0:rows_, j0:j1, :], src, st[0:rows_, 0, j0:j1].unsqueeze(2)
                                .to_broadcast([rows_, j1 - j0, T]), ALU.subtract
                            ).then_inc(read[bank(("p", b, i, 0))], 1)

                    def share(b):
                        dve.wait_ge(ex, b + 1)
                        nc.vector.tensor_reduce(st[:, 2, 0:KT], pk[:], AX.X, ALU.add).then_inc(sm, 1)
                        dve.wait_ge(sm, 2 * b + 1)
                        nc.vector.reciprocal(st[:, 3, 0:KT], st[:, 2, 0:KT]).then_inc(sm, 1)
                        dve.wait_ge(sm, 2 * b + 2)
                        nc.vector.tensor_tensor(pk[:], pk[:], st[:, 3, 0:KT].unsqueeze(2).to_broadcast([P, KT, T]),
                                                ALU.mult).then_inc(even, 1)

                    def weights(b):
                        if queries_share:
                            dve.wait_ge(w_hi, b + 1)
                            nc.vector.tensor_tensor(pT.lo[:], pk[:], pT.hi[:].bitcast(F32),
                                                    ALU.subtract).then_inc(w_lo, 1)
                            return
                        for part in PARTS:
                            i, rows_, j0, j1 = part
                            dve.wait_ge(w_hi, 2 * b + i + 1)
                            nc.vector.tensor_tensor(pT.lo[0:rows_, j0:j1, :], turned_p(dve, b, *part),
                                                    pT.hi[0:rows_, j0:j1, :].bitcast(F32), ALU.subtract
                                                    ).then_inc(read[bank(("p", b, i, 0))], 1)

                    def root(b):
                        dve.wait_ge(ex, b + 1)
                        if b >= 1:
                            dve.wait_ge(a_hi, b)
                        nc.vector.reciprocal(st[0:T, 3, 0:1], st[0:T, 2, 0:1]).then_inc(sm, 1)

                    def out_split(b):
                        dve.wait_ge(a_hi, b + 1)
                        if not queries_share:
                            nc.vector.scalar_tensor_tensor(a.lo[:, :], ps[0:T, AB, :], st[0:T, 3, 0:1],
                                                           a.hi[:, :].bitcast(F32), ALU.mult,
                                                           ALU.subtract).then_inc(a_lo, 1)
                        else:
                            dve.wait_ge(summed, b + 1)
                            nc.vector.tensor_copy(rowsum[:, b:b + 1], ps[0:T, RING, 0:1]).then_inc(a_done, 1)
                            dve.wait_ge(a_done, b + 1)
                            nc.vector.tensor_tensor(a.lo[:, :], ps[0:T, AB, :], a.hi[:, :].bitcast(F32),
                                                    ALU.subtract).then_inc(a_lo, 1)

                    def out_turned(b):
                        key = ("a", b, 0, 1)
                        src = ready(dve, key)[:, 0:C * T].rearrange("p (c t) -> p c t", c=C)
                        nc.vector.tensor_copy(aT_out.lo[:, :, b * T:(b + 1) * T], src).then_inc(read[bank(key)], 1)

                    if queries_share:
                        nc.vector.memset(pk[:, KT - 1, :], 0.0).then_inc(zeroed, 1)
                        dve.wait_ge(zeroed, 1)
                    split(0, range(KT))
                    split(1, range(KT))
                    turned(0, range(KT))
                    peaks(0)
                    for b in range(B):
                        more = b + 1 < B
                        if queries_share:
                            turned(b + 1, ahead(b + 1, 0, 1))
                            share(b)
                            turned(b + 1, ahead(b + 1, 1, 3))
                            weights(b)
                            turned(b + 1, ahead(b + 1, 3, KT))
                        else:
                            weights(b)
                            root(b)
                            turned(b + 1, ahead(b + 1, 0, KT))
                        split(b + 2, ahead(b + 2, 0, FIRST))
                        if beside is not None:
                            beside(dve, b)
                        if more:
                            peaks(b + 1)
                        split(b + 2, ahead(b + 2, FIRST, TURN))
                        out_split(b)
                        split(b + 2, ahead(b + 2, TURN, KT))
                        out_turned(b)

        ph = ExitStack()
        wv = pair("x0_wv", [P, C, D], ph)
        qT = pair("x0_qT", [P, C, N], ph)
        st1 = ExitStack()
        m0 = pair("x0_m", [P, C, D], st1)
        rv = sb("x0_rv", [P, C, D], F32, st1)
        wv0_landed, = issue_stage("in_wv0", [[(rv[:], natural(g["L0_xattn_WV"]))]])
        rows_of = lambda w: (lambda k: w[k * P:(k + 1) * P, :])
        fold_stage("m0", C, rows_of(g["L0_xattn_WQ"]), rows_of(g["L0_xattn_WK"]), m0)
        await_stage(wv0_landed)
        product_stage("turn_wv0", turn_weight(rv, wv))
        product_stage("q0", project(m0, xT, qT))
        st1.close()
        yT = xT
        st2 = ExitStack()
        context_stage("ctx0", qT, yT, False, st2, float(D) ** -0.5)
        st2.close()
        norm_stage("norm1", lambda pe, bank, b: emit_products(pe, bank, [
            p for k in range(C) for p in times(yT[:, k, b * T:(b + 1) * T], wv[:, k, :])]), x)
        ph.close()
        free_semaphores()

        late, landing = ExitStack(), ExitStack()
        decay = sb("decay", [T, T], F32, late)
        rk, rv = sb("l1_rk", [P, C, D], F32, landing)[:], sb("l1_rv", [P, C, D], F32, landing)[:]
        rd, ru, rw = (sb("l1_" + n, [P, C, P], F32, landing)[:] for n in ("rd", "ru", "rw"))
        sb("l1_pad", [P, 2 * C * N - 2 * C * D - 3 * C * P], F32, landing)
        rq, ro = sb("l1_rq", [P, C, D], F32, landing)[:], sb("l1_ro", [P, C, D], F32, landing)[:]
        in_l1, = issue_stage("in_l1", [[
            (rk, natural(g["L1_attn_Wk"])), (rv, natural(g["L1_attn_Wv"])),
            (rd, g["L1_attn_W_down_kv"].rearrange("(c p) l -> p c l", p=P)),
            (ru, g["L1_attn_W_up_k"].rearrange("l (c d) -> l c d", c=C)),
            (rw, g["L1_attn_W_up_v"].rearrange("l (c d) -> l c d", c=C)),
            (rq, natural(g["L1_attn_Wq"])), (ro, natural(g["L1_attn_Wo"])), (decay[:], g["decay"])]])
        ph = ExitStack()
        indT = sb("indT", [E, N], FR, ph)
        w_dram = nc.dram_tensor("token_weights", [E, N], F32).ap()
        gt = ExitStack()
        xf = sb("xf", [P, C, HALF], F32, gt)
        lg = sb("logits", [E, B, T], F32, gt)
        gs = sb("gate_stat", [E, 3, B], F32, gt)
        prn = sb("probs", [T, B, E], F32, gt)
        m8 = sb("top8", [T, B, E], F32, gt)
        i8 = sb("top8_index", [T, B, E], U32, gt)
        i8f = sb("top8_index_f", [T, B, E], F32, gt)
        ind = sb("chosen", [T, B, E], F32, gt)
        ind2 = sb("chosen2", [T, B, E], F32, gt)
        wn = sb("token_w", [T, B, E], F32, gt)
        wT = sb("token_wT", [E, N], F32, gt)
        chain, mm_s, lg_s, stored = sem("gate_chain"), sem("gate_mm"), sem("gate_act"), sem("gate_stored")
        with nc.Block() as block:
            CH = {}

            @block.vector
            def _(dve):
                count = [0]

                def step(ins):
                    ins.then_inc(chain, 1)
                    count[0] += 1
                    dve.wait_ge(chain, count[0])
                for h in range(2):
                    if h == 1:
                        dve.wait_ge(mm_s, 1)
                    step(nc.vector.tensor_tensor(xf[:], xT.hi[:, :, h * HALF:(h + 1) * HALF].bitcast(F32),
                                                 xT.lo[:, :, h * HALF:(h + 1) * HALF].bitcast(F32), ALU.add))
                dve.wait_ge(lg_s, 2)
                step(nc.vector.tensor_reduce(gs[:, 0, :], lg[:], AX.X, ALU.max))
                step(nc.vector.tensor_tensor(lg[:], lg[:], gs[:, 0, :].unsqueeze(2).to_broadcast([E, B, T]),
                                             ALU.subtract))
                CH["sub"] = count[0]
                dve.wait_ge(lg_s, 3)
                step(nc.vector.tensor_reduce(gs[:, 1, :], lg[:], AX.X, ALU.add))
                step(nc.vector.reciprocal(gs[:, 2, :], gs[:, 1, :]))
                step(nc.vector.tensor_tensor(lg[:], lg[:], gs[:, 2, :].unsqueeze(2).to_broadcast([E, B, T]),
                                             ALU.mult))
                CH["probs"] = count[0]
                dve.wait_ge(mm_s, 3)
                step(nc.vector.tensor_copy(prn[:].rearrange("t b e -> t (b e)"), ps[0:T, 2, 0:B * E]))
                for b in range(B):
                    step(nc.vector.max(m8[:, b, :], prn[:, b, :]))
                    step(nc.vector.max_index(i8[:, b, :], m8[:, b, :], prn[:, b, :]))
                step(nc.vector.tensor_copy(i8f[:], i8[:]))
                io = iota8[0:T, :].unsqueeze(1).to_broadcast([T, B, E])
                step(nc.vector.tensor_tensor(ind[:], io, i8f[:, :, 0:1].to_broadcast([T, B, E]), ALU.is_equal))
                step(nc.vector.tensor_tensor(ind2[:], io, i8f[:, :, 1:2].to_broadcast([T, B, E]), ALU.is_equal))
                step(nc.vector.tensor_tensor(ind[:], ind[:], ind2[:], ALU.add))
                step(nc.vector.tensor_tensor(wn[:], ind[:], prn[:], ALU.mult))
                CH["chosen"] = count[0]
                dve.wait_ge(mm_s, 4)
                for h in range(2):
                    step(nc.vector.tensor_copy(indT[:, h * HALF:(h + 1) * HALF], ps[0:E, 3 + h, 0:HALF]))
                for h in range(2):
                    step(nc.vector.tensor_copy(wT[:, h * HALF:(h + 1) * HALF], ps[0:E, 5 + h, 0:HALF]))
                CH["wT"] = count[0]

            @block.tensor
            def _(pe):
                for h in range(2):
                    pe.wait_ge(chain, h + 1)
                    mm = emit_products(nc.tensor, ps[0:E, h, 0:HALF], [(gw[:, k, :], xf[:, k, :]) for k in range(C)])
                    mm.then_inc(mm_s, 1)
                pe.wait_ge(chain, CH["probs"])
                for b in range(B):
                    mm = nc.tensor.transpose(ps[0:T, 2, b * E:(b + 1) * E], lg[:, b, :], ident[0:E, 0:E])
                mm.then_inc(mm_s, 1)
                pe.wait_ge(chain, CH["chosen"])
                for b in range(B):
                    nc.tensor.transpose(ps[0:E, 3 + b // 4, b % 4 * T:(b % 4 + 1) * T], ind[:, b, :], ident[0:T, 0:T])
                    mm = nc.tensor.transpose(ps[0:E, 5 + b // 4, b % 4 * T:(b % 4 + 1) * T], wn[:, b, :], ident[0:T, 0:T])
                mm.then_inc(mm_s, 1)

            @block.scalar
            def _(act):
                for h in range(2):
                    act.wait_ge(mm_s, h + 1)
                    nc.scalar.activation(lg[:, 4 * h:4 * h + 4, :].rearrange("e b t -> e (b t)"), ps[0:E, h, 0:HALF],
                                         ACT.Identity, bias=gb[:]).then_inc(lg_s, 1)
                act.wait_ge(chain, CH["sub"])
                nc.scalar.activation(lg[:], lg[:], ACT.Exp).then_inc(lg_s, 1)

            @block.sync
            def _(sp):
                sp.wait_ge(chain, CH["wT"])
                sp.dma_start(w_dram, wT[:]).then_inc(stored, 16)
                sp.wait_ge(stored, 16)
        gt.close()

        hA, hB = pair("hA", [P, C, N], ph), pair("hB", [P, C, N], ph)
        V = sb("v_turned", [P, C, E], F32, ph)
        Vn = pair("v_natural", [E, D], ph)

        ff = ExitStack()
        wraw = sb("ffn_raw", [P, 2, C, D], F32, ff)
        w = pair("ffn_w", [P, 2, C, D], ff)
        hf = sb("ffn_h", [P, 4, HALF], F32, ff)
        wb = sb("ffn_wb", [P, 2, N], F32, ff)
        part = sb("ffn_part", [P, 2, C, 2], F32, ff)
        (fwh, fwl, fmm, frelu, fhi, flo, fred, fsum) = (sem("ffn_" + s) for s in (
            "w_hi", "w_lo", "made", "relu", "h_hi", "h_lo", "reduced", "summed"))
        fprod, fbias = sem("ffn_product"), sem("ffn_bias")
        fl = [sem(f"ffn_landed{i}") for i in range(2)]
        fwb = [sem(f"ffn_wb_landed{i}") for i in range(2)]
        bslot = sb("ffn_bias_now", [P, 6, C], F32, ff)
        LPI = 6
        TPL = 2 * C
        expert_w = [g[f"L0_ffn_w{i}"].rearrange("e (c p) o -> e p c o", p=P) for i in (1, 2, 3)]
        srcs = [xT, hA, hB]
        LPE = 3
        HPL = 2 * (LPE - 1) * TPL
        TPR = LPI * TPL
        MADE0 = TPL + 1
        with nc.Block() as block:
            @block.sync
            def _(sp):
                for l in range(2):
                    sp.dma_start(wraw[:, l, :, :], expert_w[l][0]).then_inc(fl[l], 16)
                with sp.Fori(0, E // 2) as j:
                    sp.wait_ge(fsum, 2 * j + 1)
                    for e2 in range(2):
                        sp.dma_start(wb[:, e2, :], w_dram[bass.ds(2 * j + e2, 1), :].to_broadcast([P, N])
                                     ).then_inc(fwb[e2], 16)
                    for l in range(LPI):
                        sp.wait_ge(fwl, LPI * j + l + 1)
                        ahead = l + 2
                        sp.dma_start(wraw[:, l % 2, :, :],
                                     expert_w[ahead % LPE][bass.ds((2 * j + ahead // LPE) % E, 1)]
                                     .rearrange("a p c o -> p (a c) o")).then_inc(fl[l % 2], 16)
                for l in range(2):
                    sp.wait_ge(fl[l], 16 * (LPE * E // 2 + 1))

            @block.tensor
            def _(pe):
                pe.sem_inc(fmm, MADE0)
                with pe.Fori(0, E // 2) as j:
                    for l in range(LPI):
                        pe.wait_ge(fwl, LPI * j + l + 1)
                        src = srcs[l % LPE]
                        for n in range(TPL):
                            m, h = n // 2, n % 2
                            t = TPL * l + n
                            pe.wait_ge(frelu, TPR * j + t + 1)
                            if l % LPE and n < 2:
                                pe.wait_ge(flo, HPL * j + TPL * ((LPE - 1) * (l // LPE) + l % LPE) - 1 + n)
                            emit_products(nc.tensor, ps[:, t % 8, 0:HALF], [
                                p for k in range(C) for p in times(w[:, l % 2, k, m * P:(m + 1) * P],
                                                                   src[:, k, h * HALF:(h + 1) * HALF])
                            ]).then_inc(fmm, 1)

            @block.scalar
            def _(act):
                def split(j, l):
                    act.wait_ge(fl[l % 2], 16 * (LPI // 2 * j + l // 2 + 1))
                    act.wait_ge(fmm, MADE0 + TPR * j + TPL * (l - 1))
                    nc.scalar.activation(w.hi[:, l % 2, :, :], wraw[:, l % 2, :, :], ACT.Identity).then_inc(fwh, 1)

                act.sem_inc(frelu, 8)
                split(0, 0)
                with act.Fori(0, E // 2) as j:
                    for l in range(LPI):
                        nc.scalar.activation(
                            bslot[:, l, :].unsqueeze(2),
                            BT[:, :, bass.ds(2 * j + (ROWS[f"L0_ffn_b{l % LPE + 1}"] + l // LPE), 1)],
                            ACT.Identity).then_inc(fbias, 1)
                        act.wait_ge(fbias, LPI * j + l + 1)
                        for n in range(TPL):
                            t = TPL * l + n
                            m = n // 2
                            act.wait_ge(fmm, MADE0 + TPR * j + t + 1)
                            act.wait_ge(fhi, TPR * j + t + 1)
                            nc.scalar.activation(hf[:, t % 4, :], ps[:, t % 8, 0:HALF], ACT.Relu,
                                                 bias=bslot[:, l, m:m + 1]).then_inc(frelu, 1)
                            if n == 2:
                                split(j, l + 1)

            @block.vector
            def _(dve):
                def split(j, l):
                    dve.wait_ge(fwh, LPI * j + l + 1)
                    nc.vector.tensor_tensor(w.lo[:, l % 2, :, :], wraw[:, l % 2, :, :],
                                            w.hi[:, l % 2, :, :].bitcast(F32), ALU.subtract).then_inc(fwl, 1)

                dve.sem_inc(fhi, 4)
                dve.sem_inc(fsum, 1)
                split(0, 0)
                with dve.Fori(0, E // 2) as j:
                    for l in range(LPI):
                        for n in range(TPL):
                            t = TPL * l + n
                            m, h = n // 2, n % 2
                            dve.wait_ge(frelu, TPR * j + t + 1 + 8)
                            if l % LPE < LPE - 1:
                                dst = (hA, hB)[l % LPE][:, m, h * HALF:(h + 1) * HALF]
                                k = TPL * ((LPE - 1) * (l // LPE) + l % LPE) + n
                                nc.vector.tensor_copy(dst.hi, hf[:, t % 4, :]).then_inc(fred, 1)
                                dve.wait_ge(fred, HPL * j + k + 1)
                                nc.vector.tensor_tensor(dst.lo, hf[:, t % 4, :], dst.hi.bitcast(F32),
                                                        ALU.subtract).then_inc(flo, 1)
                                dve.wait_ge(flo, HPL * j + k + 1)
                            else:
                                e2 = l // LPE
                                k = TPL * e2 + n
                                if n == 0:
                                    dve.wait_ge(fwb[e2], 16 * (j + 1))
                                nc.vector.tensor_tensor_reduce(
                                    out=hf[:, t % 4, :], in0=hf[:, t % 4, :], in1=wb[:, e2, h * HALF:(h + 1) * HALF],
                                    scale=1.0, scalar=0.0, op0=ALU.mult, op1=ALU.add,
                                    accum_out=part[:, e2, m, h:h + 1]).then_inc(fprod, 1)
                                dve.wait_ge(fprod, 2 * TPL * j + k + 1)
                            dve.sem_inc(fhi, 1)
                            if n == 2:
                                split(j, l + 1)
                        if l % LPE == LPE - 1:
                            e2 = l // LPE
                            nc.vector.tensor_tensor(V[:, :, bass.ds(2 * j + e2, 1)], part[:, e2, :, 0:1],
                                                    part[:, e2, :, 1:2], ALU.add).then_inc(fsum, 1)
        ff.close()
        product_stage("turn_v", [flip_job([(c * P, V[:, c, :]) for c in range(C)], Vn[:, :], rows=E, cols=D)])
        norm_stage("norm2", lambda pe, bank, b: emit_products(pe, bank, [
            (indT[:, b * T:(b + 1) * T], Vn.hi[:, :]), (indT[:, b * T:(b + 1) * T], Vn.lo[:, :])]), x)
        ph.close()
        free_semaphores()

        ph = ExitStack()
        landing.close()
        qp, wo = pair("l1_q", [P, C, N], late), pair("l1_wo", [P, C, D], late)
        kf = sb("l1_k", [P, C, N], F32, ph)
        v = pair("l1_v", [T, B, NH, VW], ph)
        st1 = ExitStack()
        kv_sum = sem("kv_sum")
        with nc.Block() as block:
            @block.vector
            def _(dve):
                dve.wait_ge(*in_l1)
                nc.vector.tensor_tensor(rk, rk, rv, ALU.add).then_inc(kv_sum, 1)
                nc.vector.memset(v.hi[:, :, :, HD:HD + 1].bitcast(F32), 1.0).then_inc(kv_sum, 1)
                nc.vector.memset(v.hi[:, :, :, HD + 1:].bitcast(F32), 0.0).then_inc(kv_sum, 1)
                nc.vector.memset(v.lo[:, :, :, HD:].bitcast(F32), 0.0).then_inc(kv_sum, 1)
        pd, wd = pair("l1_pd", [P, C, LAT], st1), pair("l1_wd", [P, C, LAT], st1)
        pu, pw = pair("l1_pu", [P, 1, D], st1), pair("l1_pw", [P, 1, D], st1)
        pq = pair("l1_pq", [P, C, D], st1)
        chunked = lambda t: Pair(*(h[:, 0, :].rearrange("l (c d) -> l c d", c=C) for h in (t.hi, t.lo)))
        split_stage("split_l1", [(pd[:, :, :], rd), (chunked(pu), ru), (chunked(pw), rw), (pq[:, :, :], rq)])
        sT = pair("l1_sT", [P, C, D], st1)
        latT = pair("l1_latT", [P, 1, N], st1)
        product_stage("turn_kv", turn_weight(rk, sT))
        split_stage("split_wo1", [(wo[:, :, :], ro)])
        product_stage("down", [tile_job([p for k in range(C) for p in times(sT[:, k, m * P:(m + 1) * P], pd[:, k, :])],
                                        wd[:, m, :], cols=LAT) for m in range(C)])
        scale1 = float(1.0 / (np.sqrt(np.float32(D)) + np.float32(1e-8)))
        fjobs = lambda js, dst: [(e, vw, dst[:, n // 2, n % 2 * HALF:(n % 2 + 1) * HALF], bi, s)
                                 for n, (e, vw, d, bi, s) in enumerate(js)]
        product_stage("lat", project(wd, xT, latT, mc=1) + project(pq, xT, qp, scale=scale1))
        product_stage("up", fjobs(project(pu, latT, xT, kc=1), kf) + value_jobs(latT, pw, v, kc=1))
        st1.close()
        yT = xT
        att = ExitStack()
        bias_of = None
        attention_stage("att1", qp, kf, v, yT, 1.0, False, decay, att)
        att.close()
        ph.close()

        ph = ExitStack()
        kq = sb("kernel", [P, C * D], BF16, ph)
        sc_in, sc_k = sb("s_in", [P, 4], F32, ph), sb("s_k", [P, 4], F32, ph)
        PIECE = C * D // B
        k_tmp = [sb(f"k_quant{i}", [P, PIECE], F32, ph) for i in range(2)]
        qbk = sb("x1_qbk", [T, B], F32, ph)
        bvo = sb("x1_bvo", [P, D], F32, ph)
        ones_col = sb("ones_col", [P, 2], FR, ph)
        rowsum = sb("rowsum", [T, B], F32, ph)
        aux = sb("x1_aux", [P, 2, C], F32, ph)
        bb = sb("x1_bb", [P, 1], F32, ph)
        col = lambda key, k: BT[:, k % C, ROWS[key] + k // C:ROWS[key] + k // C + 1]
        st2 = ExitStack()
        ra, rb = sb("x1_rv", [P, HC, D], F32, st2), sb("x1_ro", [P, C, HID], F32, st2)
        in_x1, in_f8 = issue_stage("in_x1", [[(rb[:], natural(g["L1_xattn_Wo"])), (ra[:], hid(g["L1_xattn_Wv"]))], [
            (kq[:].rearrange("p (c d) -> p c d", c=C), natural(g["L1_ffn_kernel"])),
            (sc_in[:, 0:1], g["L1_ffn_input_scale"].partition_broadcast(P)),
            (sc_k[:, 0:1], g["L1_ffn_kernel_scale"].partition_broadcast(P))]])
        norm_stage("norm3", lambda pe, bank, b: emit_products(pe, bank, [
            p for k in range(C) for p in times(yT[:, k, b * T:(b + 1) * T], wo[:, k, :])]), x)
        free_semaphores()
        n1 = wo
        pv_, poT = pair("x1_pv", [P, HC, D], st2), pair("x1_poT", [P, HC, D], st2)
        bvb = pair("x1_bvb", [P, HC, P], st2)
        await_stage(in_x1)
        split_stage("split_x1b", [(pv_[:, :, :], ra[:])] + [
            (bvb[:, k, :], col("L1_xattn_bv", k).to_broadcast([P, P])) for k in range(HC)])
        product_stage("turn_wo", turn_weight(rb, poT, C, HC))
        product_stage("n1", [tile_job([p for k in range(HC) for p in times(pv_[:, k, m * P:(m + 1) * P], poT[:, k, :])],
                                      n1[:, m, :], cols=D) for m in range(C)]
                      + [tile_job([p for k in range(HC) for p in times(bvb[:, k, :], poT[:, k, :])],
                                  bvo[:, :], cols=D)])
        st2.close()
        qT = qp
        st1 = ExitStack()
        m1 = pair("x1_m", [P, C, D], st1)
        uz = pair("x1_u", [P, C, P], st1)
        ones = sem("ones1")
        with nc.Block() as block:
            @block.vector
            def _(dve):
                nc.vector.memset(ones_col[:].bitcast(F32), 1.0).then_inc(ones, 1)
                dve.wait_ge(*in_f8)
                nc.vector.reciprocal(sc_in[:, 1:2], sc_in[:, 0:1]).then_inc(ones, 1)
                nc.vector.reciprocal(sc_k[:, 1:2], sc_k[:, 0:1]).then_inc(ones, 1)
                nc.vector.tensor_tensor(sc_in[:, 2:3], sc_in[:, 0:1], sc_k[:, 0:1], ALU.mult).then_inc(ones, 1)
                nc.vector.memset(uz.hi[:].bitcast(F32), 0.0).then_inc(ones, 1)
                nc.vector.memset(uz.lo[:].bitcast(F32), 0.0).then_inc(ones, 1)
        bo1_landed, = issue_stage("in_bo1", [[(bo_rows[:], g["L1_xattn_bo"].partition_broadcast(P))]])
        extras = [(m, P, lambda k, a_, b_, m=m: b_[:, m * P:(m + 1) * P], lambda k: col("L1_xattn_bq", k))
                  for m in range(C)]
        extras += [(C + m, P, lambda k, a_, b_, m=m: a_[:, m * P:(m + 1) * P], lambda k: col("L1_xattn_bk", k))
                   for m in range(C)]
        extras += [(2 * C, P, lambda k, a_, b_: col("L1_xattn_bq", k).to_broadcast([P, P]),
                    lambda k: col("L1_xattn_bk", k))]
        fold_stage("m1", HC, rows_of(g["L1_xattn_Wq"]), rows_of(g["L1_xattn_Wk"]), m1, extras=extras, extra_jobs=[
            (aux[:, 0, :], ps[:, C, 0:C]), (uz[:, :, 0], ps[:, C, C:2 * C]), (bb[:, :], ps[:, C, 2 * C:2 * C + 1])])

        def qbk_stage():
            row = sb("x1_row", [1, N], F32, st1)
            made, kept = sem("qbk_made"), sem("qbk_kept")
            with nc.Block() as block:
                @block.tensor
                def _(pe):
                    for h in range(2):
                        emit_products(nc.tensor, ps[:, h, 0:HALF], [
                            p for k in range(C) for p in times(uz[:, k, :], xT[:, k, h * HALF:(h + 1) * HALF])
                        ]).then_inc(made, 1)
                    pe.wait_ge(kept, 2)
                    for b in range(B):
                        mm = nc.tensor.transpose(ps[0:T, 2, b:b + 1], row[0:1, b * T:(b + 1) * T], ident[0:1, 0:1])
                    mm.then_inc(made, 1)

                @block.scalar
                def _(act):
                    for h in range(2):
                        act.wait_ge(made, h + 1)
                        nc.scalar.activation(row[0:1, h * HALF:(h + 1) * HALF], ps[0:1, h, 0:HALF], ACT.Identity,
                                             bias=bb[0:1, 0:1]).then_inc(kept, 1)
                    act.wait_ge(made, 3)
                    nc.scalar.activation(qbk[:, :], ps[0:T, 2, 0:B], ACT.Identity).then_inc(kept, 1)
        qbk_stage()
        product_stage("q1", project(m1, xT, qT, bias=lambda m: aux[:, 0, m:m + 1]))
        st1.close()
        yT = xT
        st2 = ExitStack()
        k_step = sem("kernel_step")

        def kernel_piece(dve, b):
            v_, m_ = k_tmp[0][:], k_tmp[1][:]
            piece = kq[:, b * PIECE:(b + 1) * PIECE]
            steps = [lambda: nc.vector.tensor_scalar(v_, piece, sc_k[:, 1:2], None, ALU.mult)]
            steps += float8_steps(piece, v_, m_)
            for n, emit in enumerate(steps):
                if b or n:
                    dve.wait_ge(k_step, len(steps) * b + n)
                emit().then_inc(k_step, 1)

        context_stage("ctx1", qT, yT, True, st2, 64.0 ** -0.5, rowsum, qbk, bo1_landed[0], kernel_piece)
        st2.close()
        z = sb("x1_z", [T, 2, D], F32, ph)
        bias16 = sb("bias16", [P, D], BF16, ph)
        in_b16, = issue_stage("in_b16", [[(bias16[:], g["L1_ffn_bias"].partition_broadcast(P))]])
        norm_stage("norm4", lambda pe, bank, b: emit_products(pe, bank, [
            p for k in range(C) for p in times(yT[:, k, b * T:(b + 1) * T], n1[:, k, :])]), x,
            gain=lambda b: (rowsum[:, b:b + 1], bvo[0:T, :]), turned=False, z=z)
        free_semaphores()

        f8 = ExitStack()
        identB = sb("identB", [P, P], BF16, f8)
        x16 = sb("x16", [T, B, D], BF16, f8)
        xv = sb("x_scaled", [T, B, D], F32, f8)
        xm = sb("x_quant", [T, B, D], F32, f8)
        xq = sb("xq", [T, B, D], BF16, f8)
        xqT = sb("xqT", [P, C, N], BF16, f8)
        y16 = sb("y16", [T, B, D], BF16, f8)
        y32 = sb("y32", [T, B, D], F32, f8)
        rounded, scaled_in, step_s, tps, cps, mms, evs, bss, wide, ident_s = (sem("f8_" + s) for s in (
            "rounded", "scaled_in", "step", "turned", "copied", "made", "scaled", "biased", "wide", "ident"))
        steps_of = [float8_steps(xq[:, b, :], xv[:, b, :], xm[:, b, :]) for b in range(B)]
        STEPS = len(steps_of[0])
        f8_order = [(b, n) for b0 in range(0, B, 2) for n in range(STEPS) for b in (b0, b0 + 1)]
        step_at = {key: i for i, key in enumerate(f8_order)}
        with nc.Block() as block:
            @block.scalar
            def _(act):
                def scale_in(b):
                    nc.scalar.activation(x16[:, b, :], x[0:T, b, :], ACT.Identity).then_inc(rounded, 1)
                    act.wait_ge(rounded, b + 1)
                    nc.scalar.activation(xv[:, b, :], x16[:, b, :], ACT.Identity,
                                         scale=sc_in[0:T, 1:2]).then_inc(scaled_in, 1)

                for b in range(4):
                    scale_in(b)
                for b in range(B):
                    act.wait_ge(tps, b + 1)
                    bank = ps[:, b % 2, :].bitcast(BF16)
                    nc.scalar.activation(xqT[:, :, b * T:(b + 1) * T],
                                         bank[:, 0:C * T].rearrange("p (c t) -> p c t", c=C),
                                         ACT.Identity).then_inc(cps, 1)
                    if b + 4 < B:
                        scale_in(b + 4)
                    act.wait_ge(mms, b + 1)
                    nc.scalar.activation(y16[:, b, :], ps[0:T, 2 + b % 4, :], ACT.Identity,
                                         scale=sc_in[0:T, 2:3]).then_inc(evs, 1)

            @block.vector
            def _(dve):
                def finish(b):
                    dve.wait_ge(evs, b + 1)
                    nc.vector.tensor_tensor(y16[:, b, :], y16[:, b, :], bias16[0:T, :], ALU.add).then_inc(bss, 1)
                    dve.wait_ge(bss, b + 1)
                    nc.vector.tensor_tensor(y32[:, b, :], x[0:T, b, :], y16[:, b, :], ALU.add).then_inc(wide, 1)

                nc.vector.tensor_copy(identB[:], ident[:]).then_inc(ident_s, 1)
                dve.wait_ge(*in_b16)
                for b, n in f8_order:
                    if n == 0:
                        dve.wait_ge(scaled_in, b + 1)
                    else:
                        dve.wait_ge(step_s, step_at[b, n - 1] + 1)
                    steps_of[b][n]().then_inc(step_s, 1)
                    if n == STEPS - 1 and b % 2 and b >= 3:
                        finish(b - 3)
                        finish(b - 2)
                finish(B - 2)
                finish(B - 1)

            @block.tensor
            def _(pe):
                for b in range(B):
                    pe.wait_ge(step_s, step_at[b, STEPS - 1] + 1)
                    if b == 0:
                        pe.wait_ge(ident_s, 1)
                    if b >= 2:
                        pe.wait_ge(cps, b - 1)
                    bank = ps[:, b % 2, :].bitcast(BF16)
                    for c in range(C):
                        mm = nc.tensor.transpose(bank[:, c * T:(c + 1) * T], xq[:, b, c * P:(c + 1) * P],
                                                 identB[0:T, 0:T])
                    mm.then_inc(tps, 1)
                    pe.wait_ge(cps, b + 1)
                    if b >= 4:
                        pe.wait_ge(evs, b - 3)
                    emit_products(nc.tensor, ps[0:T, 2 + b % 4, :], [
                        (xqT[:, k, b * T:(b + 1) * T], kq[:, k * D:(k + 1) * D]) for k in range(C)]).then_inc(mms, 1)
        final_norm(nc, sem, ps, x, y32, stats, mv, rstd, minus_half, out)
        f8.close()
        ph.close()
        late.close()


def final_norm(nc, sem, ps, x, y, stats, mv, rstd, minus_half, out):
    stat, aggr, rooted, normed, stored = (sem("last_" + s) for s in ("stat", "aggr", "rooted", "normed", "stored"))
    with nc.Block() as block:
        @block.vector
        def _(dve):
            for b in range(B):
                nc.vector.bn_stats(stats[0:T, b, :], y[:, b, :]).then_inc(stat, 1)
                dve.wait_ge(stat, b + 1)
                nc.vector.bn_aggr(mv[0:T, b, :], stats[0:T, b, :]).then_inc(aggr, 1)
            for b in range(B):
                dve.wait_ge(rooted, 2)
                nc.vector.tensor_scalar(x[0:T, b, :], y[:, b, :], mv[0:T, b, 0:1], rstd[0:T, b:b + 1],
                                        ALU.subtract, ALU.mult).then_inc(normed, 1)

        @block.gpsimd
        def _(pool):
            pool.wait_ge(aggr, B)
            nc.gpsimd.tensor_scalar(rstd[0:T, :], mv[0:T, :, 1], EPS, None, ALU.add).then_inc(rooted, 1)
            pool.wait_ge(rooted, 1)
            nc.gpsimd.tensor_tensor(rstd[0:T, :], rstd[0:T, :], minus_half[0:T, :].to_broadcast([T, B]),
                                    ALU.pow).then_inc(rooted, 1)

        @block.sync
        def _(sp):
            for b in range(B):
                sp.wait_ge(normed, b + 1)
                sp.dma_start(out[b], x[0:T, b, :]).then_inc(stored, 16)
            sp.wait_ge(stored, 16 * B)


def kernel(**inputs):
    import concourse.bacc as _bacc
    from concourse.bass_utils import run_bass_kernel_spmd as _run

    nc = _bacc.Bacc("TRN2", target_bir_lowering=False, num_devices=1)
    arrays, args = {}, {}
    for name, value in list(inputs.items()) + list(constants().items()):
        a = np.ascontiguousarray(value)
        arrays[f"in_{name}_dram"] = a
        args[name] = nc.dram_tensor(f"in_{name}_dram", a.shape, mybir.dt.from_np(a.dtype), kind="ExternalInput").ap()
    o = nc.dram_tensor("out_0_dram", (B, T, D), F32, kind="ExternalOutput").ap()
    program(nc, args, o)
    r = _run(nc, [arrays], core_ids=[0])
    return r.results[0]["out_0_dram"]
```
